# Optimizing a Trainium2 kernel written in Bass

```python
import numpy as np
import jax
import jax.numpy as jnp

def _softmax(x, axis=-1):
    return jax.nn.softmax(x, axis=axis)

def _gelu(x):
    return jax.nn.gelu(x, approximate=True)

def _silu(x):
    return jax.nn.silu(x)

def _sigmoid(x):
    return jax.nn.sigmoid(x)

def _layernorm(x, axis=-1, eps=1e-05):
    m = jnp.mean(x, axis=axis, keepdims=True)
    v = jnp.var(x, axis=axis, keepdims=True)
    return (x - m) / jnp.sqrt(v + eps)

def _scatter_add(tgt, idx, src, axis=0):
    return tgt.at[idx].add(src)

def _segment_sum(src, seg, n):
    return jax.ops.segment_sum(src, seg, n)
kernel_name = 'mk_sandwich_d1_jaxref_r4_18d3f4'

def setup_inputs(seed: int=0):
    np.random.seed(seed)
    _w = jnp.asarray

    def _L0_attn_setup():
        import jax, jax.numpy as jnp
        import numpy as np
        EMBED_DIM = 256
        NUM_HEADS = 16
        CONTEXT = 250
        MAX_PERIOD = 10000.0
        HEAD_DIM = EMBED_DIM // NUM_HEADS

        def _apply_rope(q, k):
            B, H, T, D = q.shape
            ds = jnp.arange(D // 2, dtype=jnp.float32)
            freqs = jnp.exp(ds * (-np.log(MAX_PERIOD) * 2.0 / D))
            ts = jnp.arange(T, dtype=jnp.float32)
            ang = ts[:, None] * freqs[None, :]
            cos = jnp.cos(ang)
            sin = jnp.sin(ang)

            def rot(x):
                xr = x.reshape(B, H, T, D // 2, 2)
                xa, xb = (xr[..., 0], xr[..., 1])
                ya = xa * cos - xb * sin
                yb = xa * sin + xb * cos
                return jnp.stack([ya, yb], axis=-1).reshape(B, H, T, D)
            return (rot(q), rot(k))
        key = jax.random.key(seed)
        k1, k2, k3 = jax.random.split(key, 3)
        B, T = (2, 512)
        query = jax.random.normal(k1, (B, T, EMBED_DIM), jnp.float32)
        in_proj_w = jax.random.normal(k2, (3 * EMBED_DIM, EMBED_DIM), jnp.float32) * EMBED_DIM ** (-0.5)
        out_proj_w = jax.random.normal(k3, (EMBED_DIM, EMBED_DIM), jnp.float32) * EMBED_DIM ** (-0.5)
        return {'query': query, 'in_proj_w': in_proj_w, 'out_proj_w': out_proj_w}
    _L0_attn_in = _L0_attn_setup()

    def _L0_ffn_setup():
        import jax, jax.numpy as jnp
        import numpy as np
        D = 256
        H = 16
        DH = D // H
        DC = D // 4
        HID = 512
        G = 2
        EPG = 4
        E = G * EPG
        TOPK = 2
        EPS = 1e-06
        B, T = (2, 512)

        def _rope_sincos(t, dh):
            inv_freq = 1.0 / 10000.0 ** (jnp.arange(0, dh, 2, dtype=jnp.float32) / dh)
            ang = jnp.arange(t, dtype=jnp.float32)[:, None] * inv_freq[None, :]
            return (jnp.sin(ang), jnp.cos(ang))

        def _apply_rope(x, sin, cos):
            x1 = x[..., ::2]
            x2 = x[..., 1::2]
            r = jnp.stack([x1 * cos - x2 * sin, x1 * sin + x2 * cos], axis=-1)
            return r.reshape(x.shape)

        def _swiglu(x):
            a, b = jnp.split(x, 2, axis=-1)
            return jax.nn.silu(a) * b

        def _rmsnorm(x, w):
            return x * jax.lax.rsqrt(jnp.mean(x * x, axis=-1, keepdims=True) + EPS) * w
        key = jax.random.key(seed)
        ks = jax.random.split(key, 14)
        s = 0.02
        return {'src': jax.random.normal(ks[0], (B, T, D), jnp.float32), 'Wq': jax.random.normal(ks[1], (D, D), jnp.float32) * s, 'Wk_c': jax.random.normal(ks[2], (D, DC), jnp.float32) * s, 'Wv_c': jax.random.normal(ks[3], (D, DC), jnp.float32) * s, 'Wk': jax.random.normal(ks[4], (DC, D), jnp.float32) * s, 'Wv': jax.random.normal(ks[5], (DC, D), jnp.float32) * s, 'Wo': jax.random.normal(ks[6], (D, D), jnp.float32) * s, 'W_shared_in': jax.random.normal(ks[7], (D, 2 * HID), jnp.float32) * s, 'W_shared_out': jax.random.normal(ks[8], (HID, D), jnp.float32) * s, 'W1_shared': jax.random.normal(ks[9], (D, 2 * HID), jnp.float32) * s, 'W2_experts': jax.random.normal(ks[10], (E, HID, D), jnp.float32) * s, 'Wg_gate': jax.random.normal(ks[11], (D, G), jnp.float32) * s, 'We_gate': jax.random.normal(ks[12], (D, E), jnp.float32) * s, 'group_bias': jnp.zeros((G,), jnp.float32), 'expert_bias': jnp.zeros((E,), jnp.float32), 'norm1_w': jnp.ones((D,), jnp.float32), 'norm2_w': jnp.ones((D,), jnp.float32)}
    _L0_ffn_in = _L0_ffn_setup()
    _d = {'L0_attn_query': _L0_attn_in['query'], 'L0_attn_in_proj_w': _L0_attn_in['in_proj_w'], 'L0_attn_out_proj_w': _L0_attn_in['out_proj_w'], 'L0_ffn_Wq': _L0_ffn_in['Wq'], 'L0_ffn_Wk_c': _L0_ffn_in['Wk_c'], 'L0_ffn_Wv_c': _L0_ffn_in['Wv_c'], 'L0_ffn_Wk': _L0_ffn_in['Wk'], 'L0_ffn_Wv': _L0_ffn_in['Wv'], 'L0_ffn_Wo': _L0_ffn_in['Wo'], 'L0_ffn_W_shared_in': _L0_ffn_in['W_shared_in'], 'L0_ffn_W_shared_out': _L0_ffn_in['W_shared_out'], 'L0_ffn_W1_shared': _L0_ffn_in['W1_shared'], 'L0_ffn_W2_experts': _L0_ffn_in['W2_experts'], 'L0_ffn_Wg_gate': _L0_ffn_in['Wg_gate'], 'L0_ffn_We_gate': _L0_ffn_in['We_gate'], 'L0_ffn_group_bias': _L0_ffn_in['group_bias'], 'L0_ffn_expert_bias': _L0_ffn_in['expert_bias'], 'L0_ffn_norm1_w': _L0_ffn_in['norm1_w'], 'L0_ffn_norm2_w': _L0_ffn_in['norm2_w']}
    _x0 = _d['L0_attn_query']
    _d['L0_attn_query'] = jax.random.normal(jax.random.fold_in(jax.random.key(seed), 1), (8, 512, 256), dtype=_x0.dtype)
    del _x0
    return _d

def reference(L0_attn_query, L0_attn_in_proj_w, L0_attn_out_proj_w, L0_ffn_Wq, L0_ffn_Wk_c, L0_ffn_Wv_c, L0_ffn_Wk, L0_ffn_Wv, L0_ffn_Wo, L0_ffn_W_shared_in, L0_ffn_W_shared_out, L0_ffn_W1_shared, L0_ffn_W2_experts, L0_ffn_Wg_gate, L0_ffn_We_gate, L0_ffn_group_bias, L0_ffn_expert_bias, L0_ffn_norm1_w, L0_ffn_norm2_w):

    def _L0_attn_ref(query, in_proj_w, out_proj_w):
        import jax, jax.numpy as jnp
        import numpy as np
        EMBED_DIM = 256
        NUM_HEADS = 16
        CONTEXT = 250
        MAX_PERIOD = 10000.0
        HEAD_DIM = EMBED_DIM // NUM_HEADS

        def _apply_rope(q, k):
            B, H, T, D = q.shape
            ds = jnp.arange(D // 2, dtype=jnp.float32)
            freqs = jnp.exp(ds * (-np.log(MAX_PERIOD) * 2.0 / D))
            ts = jnp.arange(T, dtype=jnp.float32)
            ang = ts[:, None] * freqs[None, :]
            cos = jnp.cos(ang)
            sin = jnp.sin(ang)

            def rot(x):
                xr = x.reshape(B, H, T, D // 2, 2)
                xa, xb = (xr[..., 0], xr[..., 1])
                ya = xa * cos - xb * sin
                yb = xa * sin + xb * cos
                return jnp.stack([ya, yb], axis=-1).reshape(B, H, T, D)
            return (rot(q), rot(k))
        B, T, E = query.shape
        H, D = (NUM_HEADS, HEAD_DIM)
        proj = query @ in_proj_w.T
        qkv = proj.reshape(B, T, 3, H, D)
        q = jnp.transpose(qkv[:, :, 0], (0, 2, 1, 3))
        k = jnp.transpose(qkv[:, :, 1], (0, 2, 1, 3))
        v = jnp.transpose(qkv[:, :, 2], (0, 2, 1, 3))
        q, k = _apply_rope(q, k)
        pos = jnp.arange(T)
        delta = pos[:, None] - pos[None, :]
        mask = (delta >= 0) & (delta < CONTEXT)
        scores = jnp.einsum('bhtd,bhsd->bhts', q, k) * D ** (-0.5)
        scores = jnp.where(mask[None, None, :, :], scores, jnp.finfo(scores.dtype).min)
        attn = jax.nn.softmax(scores, axis=-1)
        x = jnp.einsum('bhts,bhsd->bhtd', attn, v)
        x = jnp.transpose(x, (0, 2, 1, 3)).reshape(B, T, E)
        return x @ out_proj_w.T

    def _L0_ffn_ref(src, Wq, Wk_c, Wv_c, Wk, Wv, Wo, W_shared_in, W_shared_out, W1_shared, W2_experts, Wg_gate, We_gate, group_bias, expert_bias, norm1_w, norm2_w):
        import jax, jax.numpy as jnp
        import numpy as np
        D = 256
        H = 16
        DH = D // H
        DC = D // 4
        HID = 512
        G = 2
        EPG = 4
        E = G * EPG
        TOPK = 2
        EPS = 1e-06
        B, T = (2, 512)

        def _rope_sincos(t, dh):
            inv_freq = 1.0 / 10000.0 ** (jnp.arange(0, dh, 2, dtype=jnp.float32) / dh)
            ang = jnp.arange(t, dtype=jnp.float32)[:, None] * inv_freq[None, :]
            return (jnp.sin(ang), jnp.cos(ang))

        def _apply_rope(x, sin, cos):
            x1 = x[..., ::2]
            x2 = x[..., 1::2]
            r = jnp.stack([x1 * cos - x2 * sin, x1 * sin + x2 * cos], axis=-1)
            return r.reshape(x.shape)

        def _swiglu(x):
            a, b = jnp.split(x, 2, axis=-1)
            return jax.nn.silu(a) * b

        def _rmsnorm(x, w):
            return x * jax.lax.rsqrt(jnp.mean(x * x, axis=-1, keepdims=True) + EPS) * w
        Bb, Tt, C = src.shape
        q = (src @ Wq).reshape(Bb, Tt, H, DH).transpose(0, 2, 1, 3)
        k = (src @ Wk_c @ Wk).reshape(Bb, Tt, H, DH).transpose(0, 2, 1, 3)
        v = (src @ Wv_c @ Wv).reshape(Bb, Tt, H, DH).transpose(0, 2, 1, 3)
        sin, cos = _rope_sincos(Tt, DH)
        q = _apply_rope(q, sin, cos)
        k = _apply_rope(k, sin, cos)
        attn = jnp.einsum('bhqd,bhkd->bhqk', q, k) / np.sqrt(DH).astype(np.float32)
        attn = jax.nn.softmax(attn, axis=-1)
        sa = jnp.einsum('bhqk,bhkd->bhqd', attn, v)
        sa = sa.transpose(0, 2, 1, 3).reshape(Bb, Tt, C) @ Wo
        x = _rmsnorm(src + sa, norm1_w)
        S = Bb * Tt
        flat = x.reshape(S, C)
        shared = _swiglu(flat @ W_shared_in) @ W_shared_out
        g_probs = jax.nn.softmax(flat @ Wg_gate + group_bias, -1)
        g_idx = jnp.argmax(g_probs, axis=-1)
        e_logits = flat @ We_gate + expert_bias
        e_group = jnp.arange(E) // EPG
        in_group = e_group[None, :] == g_idx[:, None]
        e_probs = jax.nn.softmax(jnp.where(in_group, e_logits, -jnp.inf), -1)
        g_prob = jnp.take_along_axis(g_probs, g_idx[:, None], axis=1)
        p_expert = e_probs * g_prob
        topv, topi = jax.lax.top_k(p_expert, TOPK)
        w = jnp.zeros((S, E), flat.dtype).at[jnp.arange(S)[:, None], topi].set(topv)
        h = _swiglu(flat @ W1_shared)
        routed = jnp.zeros_like(shared)
        for e in range(E):
            routed = routed + h @ W2_experts[e] * w[:, e:e + 1]
        out = x + (shared + routed).reshape(Bb, Tt, C)
        return _rmsnorm(out, norm2_w)
    x = L0_attn_query
    x = x + _layernorm(_L0_attn_ref(_layernorm(x, axis=-1), L0_attn_in_proj_w, L0_attn_out_proj_w), axis=-1)
    x = x + _layernorm(_L0_ffn_ref(_layernorm(x, axis=-1), L0_ffn_Wq, L0_ffn_Wk_c, L0_ffn_Wv_c, L0_ffn_Wk, L0_ffn_Wv, L0_ffn_Wo, L0_ffn_W_shared_in, L0_ffn_W_shared_out, L0_ffn_W1_shared, L0_ffn_W2_experts, L0_ffn_Wg_gate, L0_ffn_We_gate, L0_ffn_group_bias, L0_ffn_expert_bias, L0_ffn_norm1_w, L0_ffn_norm2_w), axis=-1)
    return x

_drawn_inputs = setup_inputs


def setup_inputs(seed=0):
    import zlib

    import numpy as np

    out = dict(_drawn_inputs(seed))
    spreads = {'L0_ffn_group_bias': (0.0, 0.8),
     'L0_ffn_expert_bias': (0.0, 0.8),
     'L0_ffn_norm1_w': (1.0, 0.2),
     'L0_ffn_norm2_w': (1.0, 0.2)}
    factors = {'L0_ffn_Wq': 8.0,
     'L0_ffn_Wk_c': 8.0,
     'L0_ffn_Wv_c': 8.0,
     'L0_ffn_Wk': 8.0,
     'L0_ffn_Wv': 8.0,
     'L0_ffn_Wo': 8.0,
     'L0_ffn_W_shared_in': 5.491,
     'L0_ffn_W_shared_out': 5.527,
     'L0_ffn_W1_shared': 8.0,
     'L0_ffn_W2_experts': 8.0,
     'L0_ffn_Wg_gate': 8.0,
     'L0_ffn_We_gate': 8.0}
    for name, (base, spread) in spreads.items():
        noise = np.random.default_rng([zlib.crc32(name.encode()), seed]).standard_normal(out[name].shape)
        drawn = base * np.exp(spread * noise) if base else spread * noise
        out[name] = jnp.asarray(drawn.astype(out[name].dtype))
    for name, factor in factors.items():
        out[name] = (out[name] * factor).astype(out[name].dtype)
    return out
```

```python
import numpy as np
import concourse.bass as bass
from concourse import mybir
from contextlib import ExitStack

F32 = mybir.dt.float32
F32R = mybir.dt.float32r
BF16 = mybir.dt.bfloat16
I32 = mybir.dt.int32
ALU = mybir.AluOpType
ACT = mybir.ActivationFunctionType
AX = mybir.AxisListType

P = 128
B, T, E = 8, 512, 256
H, D = 16, 16
NT = T // P
NC = E // P
CONTEXT = 250
BACK = 3
DC = E // 4
HID = 512
NH = HID // P
NG, NE, EPG = 2, 8, 4
LN_EPS, RMS_EPS = 1e-5, 1e-6
SK = 64
MROW = 3 * D
GH = 4
NGR = H // GH
UNITS = GH * NT
PSLOTS = 8
VW = 32
MASKED = -1e38
RSQRT_MAGIC = float(0x5F3759DF)


def build(nc, x, in_w, out_w, wq, wkc, wvc, wk, wv, wo, w_si, w_so, w1, w2, wgg, weg,
          g_bias, e_bias, n1w, n2w, rope, out):
    ctx = ExitStack()
    with ctx:
        def sb(name, shape, dt=F32):
            return ctx.enter_context(nc.sbuf_tensor(name, shape, dt))

        def sem(name):
            return ctx.enter_context(nc.semaphore(name))

        ident = sb("ident", [P, P])
        identb = sb("identb", [P, P], BF16)
        mask_kq = sb("mask_kq", [P, BACK * P], BF16)
        mask_qk = sb("mask_qk", [P, BACK * P], BF16)
        lower = sb("lower", [P, EPG, EPG])
        rope_cos = sb("rope_cos", [P, 2, NT, D])
        rope_sin = sb("rope_sin", [P, 2, NT, D])
        win_t = sb("win_t", [P, NC, 3 * E])
        wout_t = sb("wout_t", [P, NC, E])
        wq_s = sb("wq_s", [P, NC, E])
        wc_s = sb("wc_s", [P, NC, 2 * DC])
        wkv_s = sb("wkv_s", [P, E])
        wo_s = sb("wo_s", [P, NC, E])
        wup_s = sb("wup_s", [P, 2, NC, 2 * HID])
        wso_s = sb("wso_s", [P, NH, E])
        w2_s = sb("w2_s", [P, NH, NE, E])
        wgate_s = sb("wgate_s", [P, NC, NG + NE])
        bias_s = sb("bias_s", [P, NG + NE])
        norm_w = sb("norm_w", [P, 2, E])

        x_s = sb("x_s", [P, NT, E])
        xn = sb("xn", [P, NT, E])
        xn_t = sb("xn_t", [P, NC, T])
        rot = sb("rot", [P, 2, 2 * H, D])
        rot_b = sb("rot_b", [P, 2, 2 * H, D])
        stack = sb("stack", [P, 2, 2 * H, SK], F32R)
        q_t = sb("q_t", [P, H // 2, T], F32R)
        k_t = sb("k_t", [P, H // 2, T], F32R)
        v_s = sb("v_s", [P, NT, H, VW])
        negmax = sb("negmax", [P, 2, NT, GH])
        m_split = sb("m_split", [P, 2, NT, 2, 2, 2], F32R)
        m_t = sb("m_t", [8, 2, T])
        probs = sb("probs", [P, PSLOTS, T])
        h_t = probs[:, :, :].rearrange("p (u m) q -> p u m q", u=2)
        w_raw = probs[:, 0:4, :].rearrange("p s (r e) -> p (s r) e", e=E)
        o_t = sb("o_t", [P, 2, T])
        den = sb("den", [P, NT, GH])
        o_s = sb("o_s", [P, NT, E])
        o_tt = sb("o_tt", [P, NC, T])
        c_t = sb("c_t", [P, T])
        x1 = sb("x1", [P, NT, E])
        x2 = sb("x2", [P, NT, E])
        th = sb("th", [P, 2, T])
        sg = sb("sg", [P, 2, T])
        acc = sb("acc", [P, NT, E])
        y_s = sb("y_s", [P, NT, E])
        stats = sb("stats", [P, NT, 6])
        mv = sb("mv", [P, NT, 2])
        spare = sb("spare", [P, 1])
        var = sb("var", [P, NT])
        bits = sb("bits", [P, NT], I32)
        rstd = sb("rstd", [P, NT])
        nt1 = sb("nt1", [P, NT])
        nt2 = sb("nt2", [P, NT])
        logit = sb("logit", [P, NT, NG + NE])
        gd = sb("gd", [P, NT])
        gsel = sb("gsel", [P, NT])
        gabs = sb("gabs", [P, NT])
        gexp = sb("gexp", [P, NT])
        gprob = sb("gprob", [P, NT])
        ediff = sb("ediff", [P, NT, EPG])
        esel = sb("esel", [P, NT, EPG])
        emax = sb("emax", [P, NT])
        esub = sb("esub", [P, NT, EPG])
        eexp = sb("eexp", [P, NT, EPG])
        esum = sb("esum", [P, NT])
        egt = sb("egt", [P, NT, EPG, EPG])
        eeq = sb("eeq", [P, NT, EPG, EPG])
        rank = sb("rank", [P, NT, EPG])
        ew = sb("ew", [P, NT, EPG])
        gate = sb("gate", [P, NT, NE])

        def bank(name):
            return ctx.enter_context(nc.psum_tensor(name, [P, T], F32))

        st = [bank("st0"), bank("st1")]
        sm = [bank("sm0"), bank("sm1")]
        ot = bank("ot")
        dn = [bank("dn0"), bank("dn1"), bank("dn2")]
        wide = [st[0], st[1], sm[0], sm[1]]

        s_w = sem("weights_loaded")
        s_x = sem("x_loaded")
        s_const = sem("constants_made")
        s_wt = sem("weight_transposes_done")
        s_wc = sem("weight_transposes_copied")
        s_fill = sem("fixed_columns_filled")
        s_dve = sem("vector_step_done")
        s_pool = sem("pool_step_done")
        s_xn, N_XN = sem("normalised_rows_ready"), 3
        s_tp, N_TP = sem("row_transposes_done"), 10
        s_tc, N_TC = sem("row_transposes_copied"), 10
        s_qk, N_QK = sem("qk_projected"), 8
        s_v, N_V = sem("v_projected"), 8
        s_vc, N_VC = sem("v_copied"), 8
        s_c, N_C = sem("compressed_projected"), 1
        s_cc, N_CC = sem("compressed_copied"), 1
        s_rp, N_RP = sem("rope_products_ready"), 8
        s_rot, N_ROT = sem("rotated_ready"), 8
        s_hi, N_HI = sem("high_parts_ready"), 8
        s_lo, N_LO = sem("low_parts_ready"), 8
        s_sp, N_SP = sem("stack_transposes_done"), 32
        s_sa, N_SA = sem("stacks_copied_by_act"), 16
        s_sd, N_SD = sem("stacks_copied_by_dve"), 16
        s_sm, N_SM = sem("max_scores_done"), 2 * NGR * UNITS
        s_mx, N_MX = sem("max_taken"), 2 * NGR * UNITS
        s_ms, N_MS = sem("max_split"), 2 * NGR
        s_mp, N_MP = sem("max_transposed"), 2 * NGR
        s_mc, N_MC = sem("max_rows_copied"), 2 * NGR
        s_mr, N_MR = [sem("max_rows_placed0"), sem("max_rows_placed1")], 2 * 64 * NGR // 2
        s_st, N_ST = sem("scores_done"), 2 * NGR * UNITS
        s_ex, N_EX = sem("exps_done"), 2 * NGR * UNITS
        s_pv, N_PV = sem("values_weighed"), 2 * NGR * NT
        s_oc, N_OC = sem("outputs_copied"), 2 * NGR
        s_op, N_OP = sem("outputs_transposed"), 2 * NGR
        s_on, N_ON = sem("outputs_normalised"), 2 * NGR
        s_pj, N_PJ = sem("attention_projected"), 4
        s_res, N_RES = sem("residual_added"), 1
        s_up, N_UP = sem("hidden_projected"), 2 * NH
        s_th, N_TH = sem("tanh_ready"), 2 * NH
        s_sg, N_SG = sem("gated_half_ready"), 2 * NH
        s_ht, N_HT = sem("hidden_ready"), 2 * NH
        s_gl, N_GL = sem("gate_logits_done"), 1
        s_ge, N_GE = sem("gate_exponents_ready"), 2
        s_gx, N_GX = sem("gate_exps_done"), 2
        s_so, N_SO = sem("shared_out_done"), NT
        s_sr, N_SR = sem("shared_out_read"), NT
        s_ro, N_RO = sem("routed_out_done"), NT * NE // 2
        s_rr, N_RR = sem("routed_out_read"), NT * NE // 2
        s_y = sem("y_ready")
        s_out = sem("y_stored")
        s_yfree = sem("y_first_free")

        x_v = x.rearrange("b (t p) e -> b p t e", p=P)
        out_v = out.rearrange("b (t p) e -> b p t e", p=P)

        def qcols(j, a):
            return (j * P, min(T, (j + BACK) * P)) if a == 0 else (0, T)

        def kcols(t, a):
            return (max(0, (t + 1 - BACK) * P), (t + 1) * P) if a == 0 else (0, T)

        block = ctx.enter_context(nc.Block())

        @block.sync
        def _(sp):
            loads = [
                (w_raw[:, 0:6, :], in_w.rearrange("(r p) e -> p r e", p=P)),
                (w_raw[:, 6:8, :], out_w.rearrange("(r p) e -> p r e", p=P)),
                (rope_cos[:, :, :, :], rope[0]),
                (rope_sin[:, :, :, :], rope[1]),
                (wq_s[:, :, :], wq.rearrange("(c p) e -> p c e", p=P)),
                (wc_s[:, :, 0:DC], wkc.rearrange("(c p) e -> p c e", p=P)),
                (wc_s[:, :, DC:2 * DC], wvc.rearrange("(c p) e -> p c e", p=P)),
                (wkv_s[0:DC, :], wk),
                (wkv_s[DC:2 * DC, :], wv),
                (wo_s[:, :, :], wo.rearrange("(c p) e -> p c e", p=P)),
                (wgate_s[:, :, 0:NG], wgg.rearrange("(c p) e -> p c e", p=P)),
                (wgate_s[:, :, NG:NG + NE], weg.rearrange("(c p) e -> p c e", p=P)),
                (bias_s[:, 0:NG], g_bias.rearrange("(o n) -> o n", o=1).to_broadcast([P, NG])),
                (bias_s[:, NG:NG + NE], e_bias.rearrange("(o n) -> o n", o=1).to_broadcast([P, NE])),
                (norm_w[:, 0, :], n1w.rearrange("(o n) -> o n", o=1).to_broadcast([P, E])),
                (norm_w[:, 1, :], n2w.rearrange("(o n) -> o n", o=1).to_broadcast([P, E])),
                (wup_s[:, 0, :, :], w_si.rearrange("(c p) n -> p c n", p=P)),
                (wup_s[:, 1, :, :], w1.rearrange("(c p) n -> p c n", p=P)),
                (wso_s[:, :, :], w_so.rearrange("(c p) e -> p c e", p=P)),
            ]
            sp.dma_start(x_s[:, :, :], x_v[0]).then_inc(s_x, 16)
            for dst, src in loads:
                sp.dma_start(dst, src).then_inc(s_w, 16)
            for e in range(NE):
                sp.dma_start(w2_s[:, :, e, :], w2[e].rearrange("(c p) n -> p c n", p=P)).then_inc(s_w, 16)

            def place_maxima(i, a):
                for g in range(NGR):
                    sp.wait_ge(s_mc, i * N_MC + a * NGR + g + 1)
                    for half in range(2):
                        for part in range(2):
                            r, m = SK * half + MROW + part, 4 * half + 2 * part
                            sp.dma_start(q_t[r:r + 1, 2 * g:2 * g + 2, :].bitcast(F32),
                                         m_t[m:m + 2, g % 2, :]).then_inc(s_mr[g % 2], 16)

            def batch(i, last):
                place_maxima(i, 0)
                if not last:
                    sp.wait_ge(s_res, i * N_RES + 1)
                    sp.dma_start(x_s[:, :, :], x_v[i + 1]).then_inc(s_x, 16)
                place_maxima(i, 1)
                sp.wait_ge(s_y, i + 1)
                sp.dma_start(out_v[i], y_s[:, :, :]).then_inc(s_out, 16)

            with sp.Fori(0, B - 1) as i:
                batch(i, False)
            batch(B - 1, True)
            sp.wait_ge(s_out, 16 * B)

        N_LOADS = 19 + NE

        @block.gpsimd
        def _(pool):
            g = nc.gpsimd
            g.memset(ident[:, :], 0.0).then_inc(s_pool, 1)
            g.memset(identb[:, :], 0.0).then_inc(s_pool, 1)
            g.memset(mask_kq[:, :], 0.0).then_inc(s_pool, 1)
            g.memset(mask_qk[:, :], 0.0).then_inc(s_pool, 1)
            g.memset(lower[:, :, :], 1.0).then_inc(s_pool, 1)
            pool.wait_ge(s_pool, 5)
            for m in (ident, identb):
                g.affine_select(out=m[:, :], in_=m[:, :], compare_op=ALU.not_equal, fill=1.0, base=0,
                                pattern=[[-1, P]], channel_multiplier=1).then_inc(s_const, 1)
            g.affine_select(out=mask_kq[:, :], in_=mask_kq[:, :], compare_op=ALU.is_ge, fill=MASKED, base=0,
                            pattern=[[1, BACK * P]], channel_multiplier=-1).then_inc(s_pool, 1)
            g.affine_select(out=mask_qk[:, :], in_=mask_qk[:, :], compare_op=ALU.is_ge, fill=MASKED,
                            base=(BACK - 1) * P, pattern=[[-1, BACK * P]], channel_multiplier=1).then_inc(s_pool, 1)
            pool.wait_ge(s_pool, 7)
            g.affine_select(out=mask_kq[:, :], in_=mask_kq[:, :], compare_op=ALU.is_ge, fill=MASKED,
                            base=CONTEXT - 1, pattern=[[-1, BACK * P]], channel_multiplier=1).then_inc(s_const, 1)
            g.affine_select(out=mask_qk[:, :], in_=mask_qk[:, :], compare_op=ALU.is_ge, fill=MASKED,
                            base=CONTEXT - 1 - (BACK - 1) * P, pattern=[[1, BACK * P]],
                            channel_multiplier=-1).then_inc(s_const, 1)
            g.affine_select(out=lower[:, :, :], in_=lower[:, :, :], compare_op=ALU.is_ge, fill=0.0, base=-1,
                            pattern=[[1, EPG], [-1, EPG]], channel_multiplier=0).then_inc(s_const, 1)

            def rotate(i, a):
                for t in range(NT):
                    n, bf = a * NT + t, t % 2
                    pool.wait_ge(s_rp, i * N_RP + n + 1)
                    g.tensor_tensor(rot[:, bf], rot[:, bf], rot_b[:, bf], ALU.add).then_inc(s_rot, 1)
                    pool.wait_ge(s_hi, i * N_HI + n + 1)
                    hi = stack[:, bf].bitcast(F32)
                    g.tensor_tensor(stack[:, bf, 0:H, 2 * D:3 * D], rot[:, bf, 0:H], hi[:, 0:H, 0:D], ALU.subtract)
                    g.tensor_tensor(stack[:, bf, H:2 * H, D:2 * D], rot[:, bf, H:2 * H], hi[:, H:2 * H, 0:D],
                                    ALU.subtract).then_inc(s_lo, 1)

            with pool.Fori(0, B) as i:
                rotate(i, 0)
                rotate(i, 1)

        @block.scalar
        def _(act):
            def copy(dst, src):
                return nc.scalar.activation(dst, src, ACT.Copy)

            def split_high(i, a):
                for t in range(NT):
                    n, bf = a * NT + t, t % 2
                    act.wait_ge(s_v, i * N_V + n + 1)
                    copy(v_s[:, t, :, 0:D], dn[2][:, 0:E].rearrange("p (h d) -> p h d", h=H)).then_inc(s_vc, 1)
                    act.wait_ge(s_rot, i * N_ROT + n + 1)
                    if t >= 2:
                        act.wait_ge(s_sp, i * N_SP + a * 16 + 4 * (t - 1))
                    for src, dst in ((rot[:, bf, 0:H], stack[:, bf, 0:H, 0:2 * D].rearrange("p h (r d) -> p h r d", r=2)),
                                     (rot[:, bf, H:2 * H],
                                      stack[:, bf, H:2 * H, :].rearrange("p h (r d) -> p h r d", r=2)[:, :, :, 0:D])):
                        last = copy(dst, src.rearrange("p h (o d) -> p h o d", o=1).to_broadcast([P, H, 2, D]))
                    last.then_inc(s_hi, 1)
                    if t >= 1:
                        copy_stacks(i, a, t - 1)
                copy_stacks(i, a, NT - 1)

            def copy_stacks(i, a, t):
                for k, dst in enumerate((q_t, k_t)):
                    act.wait_ge(s_sp, i * N_SP + a * 16 + 4 * t + 2 * k + 1)
                    copy(dst[:, 0:4, t * P:(t + 1) * P],
                         wide[2 * k][:, :].rearrange("p (b q) -> p b q", b=4)).then_inc(s_sa, 1)

            def copy_maxima(i, a, g):
                act.wait_ge(s_mp, i * N_MP + a * NGR + g + 1)
                copy(m_t[:, g % 2, :], dn[0][0:8, :]).then_inc(s_mc, 1)

            def attention(i, a):
                copy_maxima(i, a, 0)
                for g in range(NGR):
                    for n in range(UNITS):
                        if n == 2 and g >= 1:
                            act.wait_ge(s_pv, i * N_PV + (a * NGR + g) * NT)
                            copy(o_t[:, (g - 1) % 2, :], ot[:, :]).then_inc(s_oc, 1)
                        u = (a * NGR + g) * UNITS + n
                        lo, hi = qcols(n // GH, a)
                        act.wait_ge(s_st, i * N_ST + u + 1)
                        if u % UNITS >= PSLOTS or g >= 1:
                            act.wait_ge(s_pv, i * N_PV + (u - PSLOTS) // GH + 1)
                        nc.scalar.activation(probs[:, n % PSLOTS, 0:hi - lo], st[n % 2][:, 0:hi - lo], ACT.Exp,
                                             scale=float(D) ** -0.5).then_inc(s_ex, 1)
                    if g + 1 < NGR:
                        copy_maxima(i, a, g + 1)
                act.wait_ge(s_pv, i * N_PV + (a * NGR + NGR) * NT)
                copy(o_t[:, (NGR - 1) % 2, :], ot[:, :]).then_inc(s_oc, 1)

            def copy_rows(i, n, dst, banks):
                for c in range(NC):
                    act.wait_ge(s_tp, i * N_TP + n * NC + c + 1)
                    copy(dst[:, c, :], banks[c][:, :]).then_inc(s_tc, 1)

            for r in range(8):
                act.wait_ge(s_wt, r + 1)
                dst = win_t[:, :, r * P:(r + 1) * P] if r < 6 else wout_t[:, :, (r - 6) * P:(r - 5) * P]
                copy(dst, wide[r % 4][:, 0:NC * P].rearrange("p (c q) -> p c q", c=NC)).then_inc(s_wc, 1)
            act.wait_ge(s_fill, 3)
            with act.Fori(0, B) as i:
                copy_rows(i, 0, xn_t, dn)
                split_high(i, 0)
                attention(i, 0)
                copy_rows(i, 1, o_tt, dn)
                copy_rows(i, 2, xn_t, dn)
                act.wait_ge(s_c, i + 1)
                copy(c_t[:, :], st[0][:, :]).then_inc(s_cc, 1)
                split_high(i, 1)
                attention(i, 1)
                copy_rows(i, 3, o_tt, dn)
                copy_rows(i, 4, xn_t, dn)
                for k, src in enumerate((gabs[:, :], esub[:, :, :])):
                    act.wait_ge(s_ge, i * N_GE + k + 1)
                    dst = (gexp[:, :], eexp[:, :, :])[k]
                    nc.scalar.activation(dst, src, ACT.Exp).then_inc(s_gx, 1)
                for n in range(2 * NH):
                    act.wait_ge(s_up, i * N_UP + n + 1)
                    if n >= 2:
                        act.wait_ge(s_sg, i * N_SG + n - 1)
                    nc.scalar.activation(th[:, n % 2, :], st[n % 2][:, :], ACT.Tanh, scale=0.5).then_inc(s_th, 1)

        @block.tensor
        def _(pe):
            mm = nc.tensor.matmul

            def transpose_rows(i, n, src, banks):
                for c in range(NC):
                    for t in range(NT):
                        last = nc.tensor.transpose(banks[c][:, t * P:(t + 1) * P], src[:, t, c * P:(c + 1) * P], ident[:, :])
                    last.then_inc(s_tp, 1)

            def project_rows(dst, w, src_t, t):
                for c in range(NC):
                    last = mm(dst, src_t[:, c, t * P:(t + 1) * P], w[:, c, :], start=(c == 0), stop=(c == NC - 1))
                return last

            def stacks(i, a, t):
                pe.wait_ge(s_lo, i * N_LO + a * NT + t + 1)
                for k in range(4):
                    if t >= 1:
                        done = a * 8 + 2 * (t - 1) + k // 2 + 1
                        if k % 2 == 0:
                            pe.wait_ge(s_sa, i * N_SA + done)
                        else:
                            pe.wait_ge(s_sd, i * N_SD + done)
                    for b in range(4):
                        pair = 2 * (4 * k + b)
                        last = nc.tensor.transpose(
                            wide[k][:, b * P:(b + 1) * P],
                            stack[:, t % 2, pair:pair + 2, :].bitcast(F32).rearrange("p h s -> p (h s)"), ident[:, :])
                    last.then_inc(s_sp, 1)

            def max_unit(i, a, g, n):
                t, h = n // GH, g * GH + n % GH
                u = (a * NGR + g) * UNITS + n
                r, b = SK * (h % 2), h // 2
                lo, hi = kcols(t, a)
                if n >= 2 or g >= 1:
                    pe.wait_ge(s_mx, i * N_MX + u - 1)
                last = mm(sm[n % 2][:, 0:hi - lo], q_t[r:r + MROW, b, t * P:(t + 1) * P], k_t[r:r + MROW, b, lo:hi],
                          start=True, stop=(a == 1))
                if a == 0:
                    last = mm(sm[n % 2][:, 0:hi - lo], identb[:, :], mask_qk[:, BACK * P - (hi - lo):BACK * P],
                              start=False, stop=True)
                last.then_inc(s_sm, 1)

            def max_rows(i, a, g):
                pe.wait_ge(s_ms, i * N_MS + a * NGR + g + 1)
                if g >= 1:
                    pe.wait_ge(s_mc, i * N_MC + a * NGR + g)
                for t in range(NT):
                    last = nc.tensor.transpose(
                        dn[0][0:8, t * P:(t + 1) * P],
                        m_split[:, g % 2, t].bitcast(F32).rearrange("p h j b -> p (h j b)"), ident[:, :])
                last.then_inc(s_mp, 1)

            def score_unit(i, a, g, n):
                j, h = n // GH, g * GH + n % GH
                u = (a * NGR + g) * UNITS + n
                r, b = SK * (h % 2), h // 2
                lo, hi = qcols(j, a)
                if n == 0:
                    pe.wait_ge(s_mr[g % 2], i * N_MR + 64 * (a * NGR // 2 + g // 2 + 1))
                if n >= 2 or g >= 1:
                    pe.wait_ge(s_ex, i * N_EX + u - 1)
                last = mm(st[n % 2][:, 0:hi - lo], k_t[r:r + SK, b, j * P:(j + 1) * P], q_t[r:r + SK, b, lo:hi],
                          start=True, stop=(a == 1))
                if a == 0:
                    last = mm(st[n % 2][:, 0:hi - lo], identb[:, :], mask_kq[:, 0:hi - lo], start=False, stop=True)
                last.then_inc(s_st, 1)

            def weigh(i, a, g, j):
                lo, hi = qcols(j, a)
                if j == 0 and g >= 1:
                    pe.wait_ge(s_oc, i * N_OC + a * NGR + g)
                for c in range(GH):
                    n = j * GH + c
                    pe.wait_ge(s_ex, i * N_EX + (a * NGR + g) * UNITS + n + 1)
                    last = mm(ot[VW * c:VW * (c + 1), lo:hi], v_s[:, j, g * GH + c, :], probs[:, n % PSLOTS, 0:hi - lo],
                              start=(j == 0), stop=(j == NT - 1), skip_group_check=True)
                last.then_inc(s_pv, 1)

            def outputs(i, a, g):
                pe.wait_ge(s_oc, i * N_OC + a * NGR + g + 1)
                if g >= 1:
                    pe.wait_ge(s_on, i * N_ON + a * NGR + g)
                for t in range(NT):
                    last = nc.tensor.transpose(dn[1][:, t * P:(t + 1) * P], o_t[:, g % 2, t * P:(t + 1) * P], ident[:, :])
                last.then_inc(s_op, 1)

            def attention(i, a):
                pe.wait_ge(s_sa, i * N_SA + (a + 1) * 8)
                pe.wait_ge(s_sd, i * N_SD + (a + 1) * 8)
                for n in range(UNITS):
                    max_unit(i, a, 0, n)
                max_rows(i, a, 0)
                for g in range(NGR):
                    for n in range(UNITS):
                        if g + 1 < NGR:
                            max_unit(i, a, g + 1, n)
                        score_unit(i, a, g, n)
                        if n % GH == 2 and n > GH:
                            weigh(i, a, g, n // GH - 1)
                        if n == 6 and g >= 1:
                            outputs(i, a, g - 1)
                    if g + 1 < NGR:
                        max_rows(i, a, g + 1)
                    weigh(i, a, g, NT - 1)
                outputs(i, a, NGR - 1)

            def project_attention(i, a, w):
                pe.wait_ge(s_on, i * N_ON + (a + 1) * NGR)
                transpose_rows(i, 1 + 2 * a, o_s, dn)
                pe.wait_ge(s_tc, i * N_TC + (2 + 2 * a) * NC)
                for m in range(2):
                    for t in (2 * m, 2 * m + 1):
                        last = project_rows(wide[m][:, (t % 2) * E:(t % 2 + 1) * E], w, o_tt, t)
                    last.then_inc(s_pj, 1)

            pe.wait_ge(s_const, 5)
            pe.wait_ge(s_w, 16 * N_LOADS)
            for r in range(8):
                if r >= 4:
                    pe.wait_ge(s_wc, r - 3)
                for c in range(NC):
                    last = nc.tensor.transpose(wide[r % 4][:, c * P:(c + 1) * P], w_raw[:, r, c * P:(c + 1) * P], ident[:, :])
                last.then_inc(s_wt, 1)
            pe.wait_ge(s_wc, 8)
            with pe.Fori(0, B) as i:
                pe.wait_ge(s_xn, i * N_XN + 1)
                transpose_rows(i, 0, xn, dn)
                pe.wait_ge(s_tc, i * N_TC + NC)
                for t in range(NT):
                    if t >= 2:
                        pe.wait_ge(s_rp, i * N_RP + t - 1)
                    project_rows(dn[t % 2][:, :], win_t[:, :, 0:2 * E], xn_t, t).then_inc(s_qk, 1)
                    if t >= 1:
                        pe.wait_ge(s_vc, i * N_VC + t)
                    project_rows(dn[2][:, 0:E], win_t[:, :, 2 * E:3 * E], xn_t, t).then_inc(s_v, 1)
                    if t >= 1:
                        stacks(i, 0, t - 1)
                stacks(i, 0, NT - 1)
                attention(i, 0)
                project_attention(i, 0, wout_t)
                pe.wait_ge(s_xn, i * N_XN + 2)
                transpose_rows(i, 2, xn, dn)
                pe.wait_ge(s_tc, i * N_TC + 3 * NC)
                for c in range(NC):
                    last = mm(st[0][:, :], wc_s[:, c, :], xn_t[:, c, :], start=(c == 0), stop=(c == NC - 1))
                last.then_inc(s_c, 1)
                pe.wait_ge(s_cc, i + 1)
                for t in range(NT):
                    if t >= 2:
                        pe.wait_ge(s_rp, i * N_RP + NT + t - 1)
                    project_rows(dn[t % 2][:, 0:E], wq_s, xn_t, t)
                    mm(dn[t % 2][:, E:2 * E], c_t[0:DC, t * P:(t + 1) * P], wkv_s[0:DC, :],
                       start=True, stop=True).then_inc(s_qk, 1)
                    if t >= 1:
                        pe.wait_ge(s_vc, i * N_VC + NT + t)
                    mm(dn[2][:, 0:E], c_t[DC:2 * DC, t * P:(t + 1) * P], wkv_s[DC:2 * DC, :],
                       start=True, stop=True).then_inc(s_v, 1)
                    if t >= 1:
                        stacks(i, 1, t - 1)
                stacks(i, 1, NT - 1)
                attention(i, 1)
                project_attention(i, 1, wo_s)
                pe.wait_ge(s_xn, i * N_XN + 3)
                transpose_rows(i, 4, x2, dn)
                pe.wait_ge(s_tc, i * N_TC + 5 * NC)
                for t in range(NT):
                    last = project_rows(dn[2][:, t * 16:t * 16 + NG + NE], wgate_s, xn_t, t)
                last.then_inc(s_gl, 1)
                for n in range(2 * NH):
                    u, m = n // NH, n % NH
                    if n >= 2:
                        pe.wait_ge(s_ht, i * N_HT + n - 1)
                    for half, dst in ((0, st[n % 2]), (1, sm[n % 2])):
                        for c in range(NC):
                            col = half * HID + m * P
                            last = mm(dst[:, :], wup_s[:, u, c, col:col + P], xn_t[:, c, :],
                                      start=(c == 0), stop=(c == NC - 1))
                    last.then_inc(s_up, 1)
                for t in range(NT):
                    if t == 0:
                        pe.wait_ge(s_ht, i * N_HT + 2 * NH)
                    if t >= 2:
                        pe.wait_ge(s_sr, i * N_SR + t - 1)
                    for m in range(NH):
                        last = mm(dn[t % 2][:, 0:E], h_t[:, 0, m, t * P:(t + 1) * P], wso_s[:, m, :],
                                  start=(m == 0), stop=(m == NH - 1))
                    last.then_inc(s_so, 1)
                    for k in range(NE // 2):
                        if t >= 1:
                            pe.wait_ge(s_rr, i * N_RR + (t - 1) * NE // 2 + k + 1)
                        for m in range(NH):
                            last = mm(wide[k][:, :], h_t[:, 1, m, t * P:(t + 1) * P],
                                      w2_s[:, m, 2 * k:2 * k + 2, :].rearrange("p e n -> p (e n)"),
                                      start=(m == 0), stop=(m == NH - 1))
                        last.then_inc(s_ro, 1)

        @block.vector
        def _(dve):
            v = nc.vector
            steps = [0]
            where = [0, 0]

            def done(ins):
                ins.then_inc(s_dve, 1)
                steps[0] += 1
                dve.wait_ge(s_dve, where[0] * where[1] + steps[0])

            def moments(rows):
                for t in range(NT):
                    last = v.bn_stats(stats[:, t, :], rows(t))
                done(last)
                v.memset(spare[:, :], 0.0)
                for t in range(NT):
                    last = v.bn_aggr(mv[:, t, :], stats[:, t, :])
                done(last)

            def inverse_root():
                done(v.tensor_scalar(bits[:, :], var[:, :].bitcast(I32), 1, None, ALU.logical_shift_right))
                done(v.tensor_scalar(rstd[:, :].bitcast(I32), bits[:, :], -1.0, RSQRT_MAGIC, ALU.mult, ALU.add))
                for _ in range(3):
                    done(v.tensor_tensor(nt1[:, :], rstd[:, :], rstd[:, :], ALU.mult))
                    done(v.scalar_tensor_tensor(nt2[:, :], nt1[:, :], -0.5, var[:, :], ALU.mult, ALU.mult))
                    done(v.scalar_tensor_tensor(rstd[:, :], nt2[:, :], 1.5, rstd[:, :], ALU.add, ALU.mult))

            def layer_scale():
                done(v.tensor_scalar(var[:, :], mv[:, :, 1], LN_EPS, None, ALU.add))
                inverse_root()

            def rms_scale():
                done(v.tensor_tensor(nt1[:, :], mv[:, :, 0], mv[:, :, 0], ALU.mult))
                done(v.scalar_tensor_tensor(var[:, :], nt1[:, :], RMS_EPS, mv[:, :, 1], ALU.add, ALU.add))
                inverse_root()

            def centred(dst, rows):
                for t in range(NT):
                    last = v.tensor_scalar(dst(t), rows(t), mv[:, t, 0:1], rstd[:, t:t + 1], ALU.subtract, ALU.mult)
                return last

            def rope_products(i, a, t):
                bf, n = t % 2, a * NT + t
                dve.wait_ge(s_qk, i * N_QK + n + 1)
                if t >= 2:
                    dve.wait_ge(s_lo, i * N_LO + n - 1)
                src = dn[t % 2][:, :].rearrange("p (h d) -> p h d", d=D)
                pairs = dn[t % 2][:, :].rearrange("p (h f o) -> p h f o", f=D // 2, o=2)
                cross = rot_b[:, bf].rearrange("p h (f o) -> p h f o", o=2)
                sin = rope_sin[:, a, t].rearrange("p (o f) -> p o f", o=2)
                v.tensor_tensor(rot[:, bf], src, rope_cos[:, a, t:t + 1, :].to_broadcast([P, 2 * H, D]), ALU.mult)
                for o in range(2):
                    last = v.tensor_tensor(cross[:, :, :, o], pairs[:, :, :, 1 - o],
                                           sin[:, o:o + 1, :].to_broadcast([P, 2 * H, D // 2]), ALU.mult)
                last.then_inc(s_rp, 1)

            def copy_stacks(i, a, t):
                for k, dst in enumerate((q_t, k_t)):
                    dve.wait_ge(s_sp, i * N_SP + a * 16 + 4 * t + 2 * k + 2)
                    v.tensor_copy(dst[:, 4:8, t * P:(t + 1) * P],
                                  wide[2 * k + 1][:, :].rearrange("p (b q) -> p b q", b=4)).then_inc(s_sd, 1)

            def heads(i, a):
                rope_products(i, a, 0)
                for t in range(NT):
                    if t + 1 < NT:
                        rope_products(i, a, t + 1)
                    copy_stacks(i, a, t)

            def take_max(i, a, g, n):
                u = (a * NGR + g) * UNITS + n
                lo, hi = kcols(n // GH, a)
                dve.wait_ge(s_sm, i * N_SM + u + 1)
                return v.tensor_reduce(negmax[:, g % 2, n // GH, n % GH:n % GH + 1], sm[n % 2][:, 0:hi - lo], AX.X,
                                       ALU.max, negate=True).then_inc(s_mx, 1)

            def split_max(i, a, g):
                dve.wait_ge(s_mx, i * N_MX + (a * NGR + g + 1) * UNITS)
                if g >= 2:
                    dve.wait_ge(s_mp, i * N_MP + a * NGR + g - 1)
                m = negmax[:, g % 2].rearrange("p t (b h) -> p t h b", b=2)
                hi = m_split[:, g % 2, :, :, 0, :]
                lo = m_split[:, g % 2, :, :, 1, :]
                done(v.tensor_copy(hi, m))
                v.tensor_tensor(lo, m, hi.bitcast(F32), ALU.subtract).then_inc(s_ms, 1)

            def normalise(i, a, g):
                dve.wait_ge(s_op, i * N_OP + a * NGR + g + 1)
                o = dn[1][:, :].rearrange("p (t h w) -> p t h w", t=NT, h=GH)
                done(v.reciprocal(den[:, :, :], o[:, :, :, D]))
                for t in range(NT):
                    last = v.tensor_tensor(
                        o_s[:, t, g * GH * D:(g + 1) * GH * D].rearrange("p (h d) -> p h d", h=GH), o[:, t, :, 0:D],
                        den[:, t].rearrange("p (h o) -> p h o", o=1).to_broadcast([P, GH, D]), ALU.mult)
                last.then_inc(s_on, 1)

            def attention(i, a):
                for g in range(NGR):
                    for n in range(UNITS):
                        take_max(i, a, g, n)
                    split_max(i, a, g)
                    if g >= 2:
                        normalise(i, a, g - 2)
                normalise(i, a, NGR - 2)
                normalise(i, a, NGR - 1)

            def projected(t):
                return wide[t // 2][:, (t % 2) * E:(t % 2 + 1) * E]

            def gates(i):
                dve.wait_ge(s_gl, i + 1)
                lg = dn[2][:, 0:NT * 16].rearrange("p (t n) -> p t n", t=NT)[:, :, 0:NG + NE]
                done(v.tensor_tensor(logit[:, :, :], lg,
                                     bias_s[:, :].rearrange("p (o n) -> p o n", o=1).to_broadcast([P, NT, NG + NE]), ALU.add))
                v.tensor_tensor(ediff[:, :, :], logit[:, :, NG + EPG:NG + NE], logit[:, :, NG:NG + EPG], ALU.subtract)
                done(v.tensor_tensor(gd[:, :], logit[:, :, 1], logit[:, :, 0], ALU.subtract))
                v.tensor_scalar(gsel[:, :], gd[:, :], 0.0, None, ALU.is_gt)
                done(v.tensor_scalar(nt1[:, :], gd[:, :], -1.0, None, ALU.mult))
                sel = gsel[:, :].rearrange("p (t o) -> p t o", o=1).to_broadcast([P, NT, EPG])
                done(v.tensor_copy(esel[:, :, :], logit[:, :, NG:NG + EPG]))
                done(v.tensor_copy(ediff[:, :, :], sel))
                v.tensor_tensor(gabs[:, :], gd[:, :], nt1[:, :], ALU.min).then_inc(s_ge, 1)
                done(v.copy_predicated(esel[:, :, :], ediff[:, :, :].bitcast(I32), logit[:, :, NG + EPG:NG + NE]))
                done(v.tensor_reduce(emax[:, :], esel[:, :, :], AX.X, ALU.max))
                v.tensor_tensor(esub[:, :, :], esel[:, :, :],
                                emax[:, :].rearrange("p (t o) -> p t o", o=1).to_broadcast([P, NT, EPG]),
                                ALU.subtract).then_inc(s_ge, 1)
                for t in range(NT):
                    one = esel[:, t].rearrange("p (e o) -> p e o", o=1).to_broadcast([P, EPG, EPG])
                    other = esel[:, t:t + 1, :].to_broadcast([P, EPG, EPG])
                    v.tensor_tensor(egt[:, t], other, one, ALU.is_gt)
                    last = v.tensor_tensor(eeq[:, t], other, one, ALU.is_equal)
                done(last)
                for t in range(NT):
                    last = v.tensor_tensor(eeq[:, t], eeq[:, t], lower[:, :, :], ALU.mult)
                done(last)
                done(v.tensor_tensor(egt[:, :, :, :], egt[:, :, :, :], eeq[:, :, :, :], ALU.add))
                done(v.tensor_reduce(rank[:, :, :], egt[:, :, :, :], AX.X, ALU.add))
                dve.wait_ge(s_gx, i * N_GX + 2)
                done(v.tensor_scalar(gprob[:, :], gexp[:, :], 1.0, None, ALU.add))
                done(v.tensor_reduce(esum[:, :], eexp[:, :, :], AX.X, ALU.add))
                done(v.tensor_tensor(gprob[:, :], gprob[:, :], esum[:, :], ALU.mult))
                done(v.reciprocal(gprob[:, :], gprob[:, :]))
                done(v.scalar_tensor_tensor(ew[:, :, :], rank[:, :, :], 2.0, eexp[:, :, :], ALU.is_lt, ALU.mult))
                done(v.tensor_tensor(ew[:, :, :], ew[:, :, :],
                                     gprob[:, :].rearrange("p (t o) -> p t o", o=1).to_broadcast([P, NT, EPG]), ALU.mult))
                done(v.tensor_tensor(gate[:, :, EPG:NE], ew[:, :, :], sel, ALU.mult))
                done(v.tensor_tensor(gate[:, :, 0:EPG], ew[:, :, :], gate[:, :, EPG:NE], ALU.subtract))

            def hidden(i, n):
                dve.wait_ge(s_th, i * N_TH + n + 1)
                v.scalar_tensor_tensor(sg[:, n % 2, :], th[:, n % 2, :], 1.0, st[n % 2][:, :], ALU.add,
                                       ALU.mult).then_inc(s_sg, 1)
                dve.wait_ge(s_sg, i * N_SG + n + 1)
                v.scalar_tensor_tensor(h_t[:, n // NH, n % NH, :], sg[:, n % 2, :], 0.5, sm[n % 2][:, :], ALU.mult,
                                       ALU.mult).then_inc(s_ht, 1)

            v.memset(v_s[:, :, :, :], 0.0)
            done(v.memset(stack[:, :, :, :].bitcast(F32), 0.0))
            v.memset(v_s[:, :, :, D:D + 1], 1.0).then_inc(s_fill, 1)
            v.memset(stack[:, :, H:2 * H, MROW:MROW + 2].bitcast(F32), 1.0).then_inc(s_fill, 1)
            v.memset(y_s[:, :, :], 0.0).then_inc(s_fill, 1)
            done(v.memset(acc[:, :, :], 0.0))
            dve.wait_ge(s_w, 16 * N_LOADS)
            dve.wait_ge(s_const, 5)
            first = steps[0]

            def batch(i):
                dve.wait_ge(s_x, i * 16 + 16)
                moments(lambda t: x_s[:, t, :])
                layer_scale()
                centred(lambda t: xn[:, t, :], lambda t: x_s[:, t, :]).then_inc(s_xn, 1)
                heads(i, 0)
                attention(i, 0)
                dve.wait_ge(s_pj, i * N_PJ + 2)
                moments(projected)
                layer_scale()
                done(centred(lambda t: acc[:, t, :], projected))
                v.tensor_tensor(x1[:, :, :], x_s[:, :, :], acc[:, :, :], ALU.add).then_inc(s_res, 1)
                dve.wait_ge(s_res, i * N_RES + 1)
                moments(lambda t: x1[:, t, :])
                layer_scale()
                centred(lambda t: xn[:, t, :], lambda t: x1[:, t, :]).then_inc(s_xn, 1)
                heads(i, 1)
                attention(i, 1)
                dve.wait_ge(s_pj, i * N_PJ + 4)
                for t in range(NT):
                    last = v.tensor_tensor(acc[:, t, :], projected(t), xn[:, t, :], ALU.add)
                done(last)
                moments(lambda t: acc[:, t, :])
                rms_scale()
                for t in range(NT):
                    last = v.scalar_tensor_tensor(x2[:, t, :], acc[:, t, :], rstd[:, t:t + 1], norm_w[:, 0, :],
                                                  ALU.mult, ALU.mult)
                last.then_inc(s_xn, 1)
                gates(i)
                for n in range(2 * NH):
                    hidden(i, n)
                for t in range(NT):
                    dve.wait_ge(s_so, i * N_SO + t + 1)
                    v.tensor_tensor(acc[:, t, :], dn[t % 2][:, 0:E], x2[:, t, :], ALU.add).then_inc(s_sr, 1)
                    dve.wait_ge(s_sr, i * N_SR + t + 1)
                    for e in range(NE):
                        k = t * NE // 2 + e // 2
                        if e % 2 == 0:
                            dve.wait_ge(s_ro, i * N_RO + k + 1)
                        add = v.scalar_tensor_tensor(acc[:, t, :], wide[e // 2][:, (e % 2) * E:(e % 2 + 1) * E],
                                                     gate[:, t, e:e + 1], acc[:, t, :], ALU.mult, ALU.add)
                        if e % 2 == 0:
                            done(add)
                        else:
                            add.then_inc(s_rr, 1)
                            dve.wait_ge(s_rr, i * N_RR + k + 1)
                moments(lambda t: acc[:, t, :])
                rms_scale()
                for t in range(NT):
                    last = v.scalar_tensor_tensor(acc[:, t, :], acc[:, t, :], rstd[:, t:t + 1], norm_w[:, 1, :],
                                                  ALU.mult, ALU.mult)
                done(last)
                moments(lambda t: acc[:, t, :])
                layer_scale()
                done(centred(lambda t: acc[:, t, :], lambda t: acc[:, t, :]))

            def finish(i):
                v.tensor_tensor(y_s[:, :, :], acc[:, :, :], x1[:, :, :], ALU.add).then_inc(s_y, 1)

            where[0], where[1] = 0, 0
            batch(0)
            finish(0)
            per_batch = steps[0] - first
            steps[0] = first
            with dve.Fori(1, B) as i:
                where[0], where[1] = i, per_batch
                batch(i)
                dve.wait_ge(s_out, i * 16)
                finish(i)
            assert steps[0] - first == per_batch


def rope_tables():
    ts = np.arange(T, dtype=np.float32)[:, None]
    ds = np.arange(D // 2, dtype=np.float32)
    out = np.zeros((2, 2, T, D), np.float32)
    for a, freqs in enumerate((np.exp(ds * np.float32(-np.log(10000.0) * 2.0 / D)),
                               np.float32(1.0) / np.float32(10000.0) ** (np.arange(0, D, 2, dtype=np.float32) / D))):
        angle = ts * freqs.astype(np.float32)[None, :]
        out[a, 0] = np.repeat(np.cos(angle), 2, axis=1)
        out[a, 1] = np.concatenate([-np.sin(angle), np.sin(angle)], axis=1)
    return np.ascontiguousarray(out.reshape(2, 2, NT, P, D).transpose(1, 3, 0, 2, 4))


_INS = ["L0_attn_query", "L0_attn_in_proj_w", "L0_attn_out_proj_w", "L0_ffn_Wq", "L0_ffn_Wk_c", "L0_ffn_Wv_c",
        "L0_ffn_Wk", "L0_ffn_Wv", "L0_ffn_Wo", "L0_ffn_W_shared_in", "L0_ffn_W_shared_out", "L0_ffn_W1_shared",
        "L0_ffn_W2_experts", "L0_ffn_Wg_gate", "L0_ffn_We_gate", "L0_ffn_group_bias", "L0_ffn_expert_bias",
        "L0_ffn_norm1_w", "L0_ffn_norm2_w"]


def kernel(**inputs):
    import concourse.bacc as bacc
    from concourse.bass_utils import run_bass_kernel_spmd

    nc = bacc.Bacc("TRN2", target_bir_lowering=False, num_devices=1)
    arrays = {f"in_{n}": np.ascontiguousarray(inputs[n]) for n in _INS}
    arrays["in_rope"] = rope_tables()
    args = [nc.dram_tensor(n, a.shape, mybir.dt.from_np(a.dtype), kind="ExternalInput").ap() for n, a in arrays.items()]
    out = nc.dram_tensor("out_0", (B, T, E), F32, kind="ExternalOutput").ap()
    build(nc, *args, out)
    r = run_bass_kernel_spmd(nc, [arrays], core_ids=[0])
    return r.results[0]["out_0"]
```

```python
import numpy as np
import concourse.bass as bass
from concourse import mybir
from contextlib import ExitStack

F32 = mybir.dt.float32
F32R = mybir.dt.float32r
BF16 = mybir.dt.bfloat16
I32 = mybir.dt.int32
ALU = mybir.AluOpType
ACT = mybir.ActivationFunctionType
AX = mybir.AxisListType

P = 128
B, T, E = 8, 512, 256
H, D = 16, 16
NT = T // P
NC = E // P
CONTEXT = 250
BACK = 3
DC = E // 4
HID = 512
NH = HID // P
NG, NE, EPG = 2, 8, 4
LN_EPS, RMS_EPS = 1e-5, 1e-6
SK = 64
MROW = 3 * D
GH = 4
NGR = H // GH
UNITS = GH * NT
PSLOTS = 8
VW = 32
MASKED = -1e38
OUTS = NT + NT * NE // 2
LEAD = 24
ALL = NGR * UNITS
HIDDEN_AT = {-14: 0, -2: 1, 8: 2, 18: 3, 28: 4, 38: 5, 48: 6, 58: 7}
OUT_FIRST, OUT_SECOND, OUT_LAST = range(0, 5), range(5, 8), range(15, OUTS)
OUT_AT = {-14: 8, -2: 9, 10: 10, 22: 11, 34: 12, 46: 13, 58: 14}
ACT_LAG, DVE_LAG = 1, 2
FINISH_AT = {12: 0, 22: 1, 32: 2, 42: 3}
SOURCE_AT = {40: 0, 52: 1}
ROWS_AT = 2
RSQRT_MAGIC = float(0x5F3759DF)


def build(nc, x, in_w, out_w, wq, wkc, wvc, wk, wv, wo, w_si, w_so, w1, w2, wgg, weg,
          g_bias, e_bias, n1w, n2w, rope, out):
    ctx = ExitStack()
    with ctx:
        def sb(name, shape, dt=F32):
            return ctx.enter_context(nc.sbuf_tensor(name, shape, dt))

        def sem(name):
            return ctx.enter_context(nc.semaphore(name))

        ident = sb("ident", [P, P])
        identb = sb("identb", [P, P], BF16)
        mask_kq = sb("mask_kq", [P, BACK * P], BF16)
        mask_qk = sb("mask_qk", [P, BACK * P], BF16)
        lower = sb("lower", [P, EPG, EPG])
        rope_cos = sb("rope_cos", [P, 2, NT, D])
        rope_sin = sb("rope_sin", [P, 2, NT, D])
        win_t = sb("win_t", [P, NC, 3 * E])
        wout_t = sb("wout_t", [P, NC, E])
        wq_s = sb("wq_s", [P, NC, E])
        wc_s = sb("wc_s", [P, NC, 2 * DC])
        wkv_s = sb("wkv_s", [P, E])
        wo_s = sb("wo_s", [P, NC, E])
        wup_s = sb("wup_s", [P, 2, NC, 2 * HID])
        wso_s = sb("wso_s", [P, NH, E])
        w2_s = sb("w2_s", [P, NH, NE, E])
        wgate_s = sb("wgate_s", [P, NC, NG + NE])
        bias_s = sb("bias_s", [P, NG + NE])
        norm_w = sb("norm_w", [P, 2, E])

        x_s = sb("x_s", [P, NT, E])
        xa = sb("xa", [P, NT, E])
        xn_t = sb("xn_t", [P, NC, T])
        rot = sb("rot", [P, 2, 2 * H, D])
        rot_b = sb("rot_b", [P, 2 * H, D])
        stack = sb("stack", [P, 2, 2 * H, SK], F32R)
        q_t = sb("q_t", [P, H // 2, T], F32R)
        k_t = sb("k_t", [P, H // 2, T], F32R)
        v_s = sb("v_s", [P, NT, H, VW])
        negmax = sb("negmax", [P, 2, NT, GH])
        m_split = sb("m_split", [P, 2, NT, 2, 2, 2], F32R)
        m_t = sb("m_t", [8, T])
        probs = sb("probs", [P, PSLOTS, T])
        w_raw = probs[:, 0:4, :].rearrange("p s (r e) -> p (s r) e", e=E)
        o_t = sb("o_t", [P, T])
        den = sb("den", [P, NT, GH])
        o_s = sb("o_s", [P, NT, E])
        x1 = sb("x1", [P, NT, E])
        x1_kept = sb("x1_kept", [P, NT, E])
        x2 = sb("x2", [P, NT, E])
        xn = x2
        th = sb("th", [P, T])
        c_t = th
        sg = sb("sg", [P, T])
        h_t = sb("h_t", [P, 2, NH, T])
        acc = sb("acc", [P, NT, E])
        stats = sb("stats", [P, NT, 6])
        mv = sb("mv", [P, NT, 2])
        spare = sb("spare", [P, 1])
        var = sb("var", [P, NT])
        bits = sb("bits", [P, NT], I32)
        rstd = sb("rstd", [P, NT])
        nt1 = sb("nt1", [P, NT])
        nt2 = sb("nt2", [P, NT])
        logit = sb("logit", [P, NT, NG + NE])
        gd = sb("gd", [P, NT])
        gsel = sb("gsel", [P, NT])
        gabs = sb("gabs", [P, NT])
        gexp = sb("gexp", [P, NT])
        gprob = sb("gprob", [P, NT])
        ediff = sb("ediff", [P, NT, EPG])
        esel = sb("esel", [P, NT, EPG])
        emax = sb("emax", [P, NT])
        esub = sb("esub", [P, NT, EPG])
        eexp = sb("eexp", [P, NT, EPG])
        esum = sb("esum", [P, NT])
        egt = sb("egt", [P, NT, EPG, EPG])
        eeq = sb("eeq", [P, NT, EPG, EPG])
        rank = sb("rank", [P, NT, EPG])
        ew = sb("ew", [P, NT, EPG])
        gate = sb("gate", [P, NT, NE])

        def bank(name):
            return ctx.enter_context(nc.psum_tensor(name, [P, T], F32))

        st = [bank("st0"), bank("st1")]
        sm = [bank("sm0"), bank("sm1")]
        ot = bank("ot")
        dn = bank("dn")
        fb = [bank("fb0"), bank("fb1")]
        pair = [dn, ot]
        tri = [st[0], st[1], sm[0]]
        vb = sm[1]

        s_w = sem("weights_loaded")
        s_x = sem("x_loaded")
        s_const = sem("constants_made")
        s_wt = sem("weight_transposes_done")
        s_wc = sem("weight_transposes_copied")
        s_fill = sem("fixed_columns_filled")
        s_dve = sem("vector_step_done")
        s_pool = sem("pool_step_done")
        s_xa = sem("first_source_ready")
        s_xn = sem("second_source_ready")
        s_x2 = sem("expert_source_ready")
        s_tp, N_TP = sem("row_transposes_done"), 4 * NC
        s_tc, N_TC = sem("row_transposes_copied"), 4 * NC
        s_fp, N_FP = sem("expert_rows_transposed"), NC
        s_fc, N_FC = sem("expert_rows_copied"), NC
        s_qk, N_QK = sem("qk_projected"), 2 * NT
        s_v, N_V = sem("v_projected"), 2 * NT
        s_vc, N_VC = sem("v_copied"), 2 * NT
        s_c, s_cc = sem("compressed_projected"), sem("compressed_copied")
        s_rp, N_RP = sem("rope_products_ready"), 2 * NT
        s_rot, N_ROT = sem("rotated_ready"), 2 * NT
        s_hi, N_HI = sem("high_parts_ready"), 2 * NT
        s_lo, N_LO = sem("low_parts_ready"), 2 * NT
        s_sp, N_SP = sem("stack_transposes_done"), 8 * NT
        s_sa, N_SA = sem("stacks_copied_by_act"), 4 * NT
        s_sd, N_SD = sem("stacks_copied_by_dve"), 4 * NT
        s_sm, N_SM = sem("max_scores_done"), 2 * NGR * UNITS
        s_mx, N_MX = sem("max_taken"), 2 * NGR * UNITS
        s_ms, N_MS = sem("max_split"), 2 * NGR
        s_mp, N_MP = sem("max_transposed"), 2 * NGR
        s_mc, N_MC = sem("max_rows_copied"), 2 * NGR
        s_mr, N_MR = [sem("max_rows_placed0"), sem("max_rows_placed1")], 2 * 64 * NGR // 2
        s_st, N_ST = sem("scores_done"), 2 * NGR * UNITS
        s_ex, N_EX = sem("exps_done"), 2 * NGR * UNITS
        s_pv, N_PV = sem("values_weighed"), 2 * NGR * NT
        s_oc, N_OC = sem("outputs_copied"), 2 * NGR
        s_op, N_OP = sem("outputs_transposed"), 2 * NGR
        s_on, N_ON = sem("outputs_normalised"), 2 * NGR
        s_pj, N_PJ = sem("attention_projected"), 4
        s_pr, N_PR = sem("projection_read"), 2
        s_res = sem("first_residual_added")
        s_gl, s_gr = sem("gate_logits_done"), sem("gate_logits_read")
        s_ge, N_GE = sem("gate_exponents_ready"), 2
        s_gx, N_GX = sem("gate_exps_done"), 2
        s_up, N_UP = sem("hidden_projected"), 2 * NH
        s_th, N_TH = sem("tanh_ready"), 2 * NH
        s_sg, N_SG = sem("gated_half_ready"), 2 * NH
        s_ht, N_HT = sem("hidden_ready"), 2 * NH
        s_eo, N_EO = sem("expert_out_done"), OUTS
        s_er, N_ER = sem("expert_out_read"), OUTS
        s_xk, s_xf = sem("x1_kept"), sem("x1_kept_free")
        s_y = sem("y_ready")
        s_yfree = sem("y_stored_or_first_free")

        x_v = x.rearrange("b (t p) e -> b p t e", p=P)
        out_v = out.rearrange("b (t p) e -> b p t e", p=P)

        def qcols(j, a):
            return (j * P, min(T, (j + BACK) * P)) if a == 0 else (0, T)

        def kcols(t, a):
            return (max(0, (t + 1 - BACK) * P), (t + 1) * P) if a == 0 else (0, T)

        block = ctx.enter_context(nc.Block())


        @block.sync
        def _(sp):
            loads = [
                (w_raw[:, 0:6, :], in_w.rearrange("(r p) e -> p r e", p=P)),
                (w_raw[:, 6:8, :], out_w.rearrange("(r p) e -> p r e", p=P)),
                (rope_cos[:, :, :, :], rope[0]),
                (rope_sin[:, :, :, :], rope[1]),
                (wq_s[:, :, :], wq.rearrange("(c p) e -> p c e", p=P)),
                (wc_s[:, :, 0:DC], wkc.rearrange("(c p) e -> p c e", p=P)),
                (wc_s[:, :, DC:2 * DC], wvc.rearrange("(c p) e -> p c e", p=P)),
                (wkv_s[0:DC, :], wk),
                (wkv_s[DC:2 * DC, :], wv),
                (wo_s[:, :, :], wo.rearrange("(c p) e -> p c e", p=P)),
                (wgate_s[:, :, 0:NG], wgg.rearrange("(c p) e -> p c e", p=P)),
                (wgate_s[:, :, NG:NG + NE], weg.rearrange("(c p) e -> p c e", p=P)),
                (bias_s[:, 0:NG], g_bias.rearrange("(o n) -> o n", o=1).to_broadcast([P, NG])),
                (bias_s[:, NG:NG + NE], e_bias.rearrange("(o n) -> o n", o=1).to_broadcast([P, NE])),
                (norm_w[:, 0, :], n1w.rearrange("(o n) -> o n", o=1).to_broadcast([P, E])),
                (norm_w[:, 1, :], n2w.rearrange("(o n) -> o n", o=1).to_broadcast([P, E])),
                (wup_s[:, 0, :, :], w_si.rearrange("(c p) n -> p c n", p=P)),
                (wup_s[:, 1, :, :], w1.rearrange("(c p) n -> p c n", p=P)),
                (wso_s[:, :, :], w_so.rearrange("(c p) e -> p c e", p=P)),
            ]
            sp.dma_start(x_s[:, :, :], x_v[0]).then_inc(s_x, 16)
            for dst, src in loads:
                sp.dma_start(dst, src).then_inc(s_w, 16)
            for e in range(NE):
                sp.dma_start(w2_s[:, :, e, :], w2[e].rearrange("(c p) n -> p c n", p=P)).then_inc(s_w, 16)

            def place_maxima(i, a):
                for g in range(NGR):
                    sp.wait_ge(s_mc, i * N_MC + a * NGR + g + 1)
                    for half in range(2):
                        for part in range(2):
                            r, m = SK * half + MROW + part, 4 * half + 2 * part
                            sp.dma_start(q_t[r:r + 1, 2 * g:2 * g + 2, :].bitcast(F32),
                                         m_t[m:m + 2, :]).then_inc(s_mr[g % 2], 16)

            def store(f):
                sp.wait_ge(s_y, f + 1)
                sp.dma_start(out_v[f], acc[:, :, :]).then_inc(s_yfree, 16)

            def keep_x1(f):
                sp.wait_ge(s_xf, f + 1)
                sp.wait_ge(s_res, f + 1)
                sp.dma_start(x1_kept[:, :, :], x1[:, :, :]).then_inc(s_xk, 16)

            def batch(i, f, e, more):
                place_maxima(i, 0)
                if e is not None:
                    store(e)
                if f is not None:
                    keep_x1(f)
                if more:
                    sp.wait_ge(s_res, i + 1)
                    sp.dma_start(x_s[:, :, :], x_v[i + 1]).then_inc(s_x, 16)
                place_maxima(i, 1)

            batch(0, None, None, True)
            batch(1, 0, None, True)
            with sp.Fori(2, B - 1) as i:
                batch(i, i - 1, i - 2, True)
            batch(B - 1, B - 2, B - 3, False)
            store(B - 2)
            keep_x1(B - 1)
            store(B - 1)
            sp.wait_ge(s_yfree, 16 * B + 16)

        N_LOADS = 19 + NE

        @block.gpsimd
        def _(pool):
            g = nc.gpsimd
            g.memset(ident[:, :], 0.0).then_inc(s_pool, 1)
            g.memset(identb[:, :], 0.0).then_inc(s_pool, 1)
            g.memset(mask_kq[:, :], 0.0).then_inc(s_pool, 1)
            g.memset(mask_qk[:, :], 0.0).then_inc(s_pool, 1)
            g.memset(lower[:, :, :], 1.0).then_inc(s_pool, 1)
            pool.wait_ge(s_pool, 5)
            for m in (ident, identb):
                g.affine_select(out=m[:, :], in_=m[:, :], compare_op=ALU.not_equal, fill=1.0, base=0,
                                pattern=[[-1, P]], channel_multiplier=1).then_inc(s_const, 1)
            g.affine_select(out=mask_kq[:, :], in_=mask_kq[:, :], compare_op=ALU.is_ge, fill=MASKED, base=0,
                            pattern=[[1, BACK * P]], channel_multiplier=-1).then_inc(s_pool, 1)
            g.affine_select(out=mask_qk[:, :], in_=mask_qk[:, :], compare_op=ALU.is_ge, fill=MASKED,
                            base=(BACK - 1) * P, pattern=[[-1, BACK * P]], channel_multiplier=1).then_inc(s_pool, 1)
            pool.wait_ge(s_pool, 7)
            g.affine_select(out=mask_kq[:, :], in_=mask_kq[:, :], compare_op=ALU.is_ge, fill=MASKED,
                            base=CONTEXT - 1, pattern=[[-1, BACK * P]], channel_multiplier=1).then_inc(s_const, 1)
            g.affine_select(out=mask_qk[:, :], in_=mask_qk[:, :], compare_op=ALU.is_ge, fill=MASKED,
                            base=CONTEXT - 1 - (BACK - 1) * P, pattern=[[1, BACK * P]],
                            channel_multiplier=-1).then_inc(s_const, 1)
            g.affine_select(out=lower[:, :, :], in_=lower[:, :, :], compare_op=ALU.is_ge, fill=0.0, base=-1,
                            pattern=[[1, EPG], [-1, EPG]], channel_multiplier=0).then_inc(s_const, 1)

            def rotate(i, a):
                for t in range(NT):
                    n, bf = a * NT + t, t % 2
                    pool.wait_ge(s_rp, i * N_RP + n + 1)
                    g.tensor_tensor(rot[:, bf], rot[:, bf], rot_b[:, :, :], ALU.add).then_inc(s_rot, 1)
                    pool.wait_ge(s_hi, i * N_HI + n + 1)
                    hi = stack[:, bf].bitcast(F32)
                    g.tensor_tensor(stack[:, bf, 0:H, 2 * D:3 * D], rot[:, bf, 0:H], hi[:, 0:H, 0:D], ALU.subtract)
                    g.tensor_tensor(stack[:, bf, H:2 * H, D:2 * D], rot[:, bf, H:2 * H], hi[:, H:2 * H, 0:D],
                                    ALU.subtract).then_inc(s_lo, 1)

            rotate(0, 0)
            rotate(0, 1)
            with pool.Fori(1, B) as i:
                rotate(i, 0)
                rotate(i, 1)

        @block.scalar
        def _(act):
            def copy(dst, src):
                return nc.scalar.activation(dst, src, ACT.Copy)

            def split_high(i, a):
                for t in range(NT):
                    n, bf = a * NT + t, t % 2
                    act.wait_ge(s_v, i * N_V + n + 1)
                    copy(v_s[:, t, :, 0:D], vb[:, 0:E].rearrange("p (h d) -> p h d", h=H)).then_inc(s_vc, 1)
                    act.wait_ge(s_rot, i * N_ROT + n + 1)
                    if t >= 2:
                        act.wait_ge(s_sp, i * N_SP + a * 16 + 4 * (t - 1))
                    for src, dst in ((rot[:, bf, 0:H], stack[:, bf, 0:H, 0:2 * D].rearrange("p h (r d) -> p h r d", r=2)),
                                     (rot[:, bf, H:2 * H],
                                      stack[:, bf, H:2 * H, :].rearrange("p h (r d) -> p h r d", r=2)[:, :, :, 0:D])):
                        last = copy(dst, src.rearrange("p h (o d) -> p h o d", o=1).to_broadcast([P, H, 2, D]))
                    last.then_inc(s_hi, 1)
                    if t >= 1:
                        copy_stacks(i, a, t - 1)
                copy_stacks(i, a, NT - 1)

            def copy_stacks(i, a, t):
                for k, dst in ((0, q_t), (2, k_t)):
                    act.wait_ge(s_sp, i * N_SP + a * 16 + 4 * t + k + 1)
                    copy(dst[:, 0:4, t * P:(t + 1) * P],
                         tri[(4 * t + k) % 3][:, :].rearrange("p (b q) -> p b q", b=4)).then_inc(s_sa, 1)

            def copy_maxima(i, a, g):
                act.wait_ge(s_mp, i * N_MP + a * NGR + g + 1)
                copy(m_t[:, :], dn[0:8, :]).then_inc(s_mc, 1)

            def copy_outputs(i, a, g):
                act.wait_ge(s_pv, i * N_PV + (a * NGR + g + 1) * NT)
                copy(o_t[:, :], ot[:, :]).then_inc(s_oc, 1)

            def tanh(f, n):
                act.wait_ge(s_up, f * N_UP + n + 1)
                if n >= 1:
                    act.wait_ge(s_sg, f * N_SG + n)
                nc.scalar.activation(th[:, :], fb[0][:, :], ACT.Tanh, scale=0.5).then_inc(s_th, 1)

            def gate_exps(f):
                for k, src in enumerate((gabs[:, :], esub[:, :, :])):
                    act.wait_ge(s_ge, f * N_GE + k + 1)
                    dst = (gexp[:, :], eexp[:, :, :])[k]
                    nc.scalar.activation(dst, src, ACT.Exp).then_inc(s_gx, 1)

            def attention(i, f, a):
                for m in range(-LEAD, ALL):
                    if m >= 0:
                        g, n = divmod(m, UNITS)
                        if n == 2 and g >= 1:
                            copy_outputs(i, a, g - 1)
                        u = a * ALL + m
                        lo, hi = qcols(n // GH, a)
                        act.wait_ge(s_st, i * N_ST + u + 1)
                        if m >= PSLOTS:
                            act.wait_ge(s_pv, i * N_PV + (u - PSLOTS) // GH + 1)
                        nc.scalar.activation(probs[:, n % PSLOTS, 0:hi - lo], st[n % 2][:, 0:hi - lo], ACT.Exp,
                                             scale=float(D) ** -0.5).then_inc(s_ex, 1)
                    if (m + LEAD) % UNITS == ROWS_AT + ACT_LAG and UNITS < m + LEAD < ALL + UNITS:
                        copy_maxima(i, a, (m + LEAD) // UNITS - 1)
                    if f is not None and a == 0 and m - ACT_LAG in HIDDEN_AT:
                        tanh(f, HIDDEN_AT[m - ACT_LAG])
                copy_outputs(i, a, NGR - 1)

            def copy_rows(i, n):
                for c in range(NC):
                    act.wait_ge(s_tp, i * N_TP + n * NC + c + 1)
                    copy(xn_t[:, c, :], pair[c][:, :]).then_inc(s_tc, 1)

            def copy_expert_rows(f):
                for c in range(NC):
                    act.wait_ge(s_fp, f * N_FP + c + 1)
                    copy(xn_t[:, c, :], fb[c][:, :]).then_inc(s_fc, 1)

            def batch(i, f):
                copy_rows(i, 0)
                split_high(i, 0)
                if f is not None:
                    copy_expert_rows(f)
                    gate_exps(f)
                attention(i, f, 0)
                copy_rows(i, 1)
                copy_rows(i, 2)
                act.wait_ge(s_c, i + 1)
                copy(c_t[:, :], st[0][:, :]).then_inc(s_cc, 1)
                split_high(i, 1)
                attention(i, f, 1)
                copy_rows(i, 3)

            for r in range(8):
                act.wait_ge(s_wt, r + 1)
                dst = win_t[:, :, r * P:(r + 1) * P] if r < 6 else wout_t[:, :, (r - 6) * P:(r - 5) * P]
                copy(dst, tri[r % 3][:, 0:NC * P].rearrange("p (c q) -> p c q", c=NC)).then_inc(s_wc, 1)
            act.wait_ge(s_fill, 2)
            batch(0, None)
            with act.Fori(1, B) as i:
                batch(i, i - 1)
            copy_expert_rows(B - 1)
            gate_exps(B - 1)
            for n in range(2 * NH):
                tanh(B - 1, n)

        @block.tensor
        def _(pe):
            mm = nc.tensor.matmul

            def transpose_rows(src, banks, signal):
                for c in range(NC):
                    for t in range(NT):
                        last = nc.tensor.transpose(banks[c][:, t * P:(t + 1) * P], src[:, t, c * P:(c + 1) * P], ident[:, :])
                    last.then_inc(signal, 1)

            def project_rows(dst, w, src_t, t):
                for c in range(NC):
                    last = mm(dst, src_t[:, c, t * P:(t + 1) * P], w[:, c, :], start=(c == 0), stop=(c == NC - 1))
                return last

            def stacks(i, a, t):
                pe.wait_ge(s_lo, i * N_LO + a * NT + t + 1)
                for k in range(4):
                    before = 4 * t + k - 3
                    if before >= 0:
                        read = a * 8 + before // 2 + 1
                        if before % 2 == 0:
                            pe.wait_ge(s_sa, i * N_SA + read)
                        else:
                            pe.wait_ge(s_sd, i * N_SD + read)
                    for b in range(4):
                        pr = 2 * (4 * k + b)
                        last = nc.tensor.transpose(
                            tri[(4 * t + k) % 3][:, b * P:(b + 1) * P],
                            stack[:, t % 2, pr:pr + 2, :].bitcast(F32).rearrange("p h s -> p (h s)"), ident[:, :])
                    last.then_inc(s_sp, 1)

            def max_unit(i, a, g, n):
                t, h = n // GH, g * GH + n % GH
                u = (a * NGR + g) * UNITS + n
                r, b = SK * (h % 2), h // 2
                lo, hi = kcols(t, a)
                if n >= 2 or g >= 1:
                    pe.wait_ge(s_mx, i * N_MX + u - 1)
                last = mm(sm[n % 2][:, 0:hi - lo], q_t[r:r + MROW, b, t * P:(t + 1) * P], k_t[r:r + MROW, b, lo:hi],
                          start=True, stop=(a == 1))
                if a == 0:
                    last = mm(sm[n % 2][:, 0:hi - lo], identb[:, :], mask_qk[:, BACK * P - (hi - lo):BACK * P],
                              start=False, stop=True)
                last.then_inc(s_sm, 1)

            def max_rows(i, a, g):
                pe.wait_ge(s_ms, i * N_MS + a * NGR + g + 1)
                if g >= 2:
                    pe.wait_ge(s_on, i * N_ON + a * NGR + g - 1)
                for t in range(NT):
                    last = nc.tensor.transpose(
                        dn[0:8, t * P:(t + 1) * P],
                        m_split[:, g % 2, t].bitcast(F32).rearrange("p h j b -> p (h j b)"), ident[:, :])
                last.then_inc(s_mp, 1)

            def score_unit(i, a, g, n):
                j, h = n // GH, g * GH + n % GH
                u = (a * NGR + g) * UNITS + n
                r, b = SK * (h % 2), h // 2
                lo, hi = qcols(j, a)
                if n == 0:
                    pe.wait_ge(s_mr[g % 2], i * N_MR + 64 * (a * NGR // 2 + g // 2 + 1))
                if n >= 2 or g >= 1:
                    pe.wait_ge(s_ex, i * N_EX + u - 1)
                last = mm(st[n % 2][:, 0:hi - lo], k_t[r:r + SK, b, j * P:(j + 1) * P], q_t[r:r + SK, b, lo:hi],
                          start=True, stop=(a == 1))
                if a == 0:
                    last = mm(st[n % 2][:, 0:hi - lo], identb[:, :], mask_kq[:, 0:hi - lo], start=False, stop=True)
                last.then_inc(s_st, 1)

            def weigh(i, a, g, j):
                lo, hi = qcols(j, a)
                if j == 0 and g >= 1:
                    pe.wait_ge(s_oc, i * N_OC + a * NGR + g)
                for c in range(GH):
                    n = j * GH + c
                    pe.wait_ge(s_ex, i * N_EX + (a * NGR + g) * UNITS + n + 1)
                    last = mm(ot[VW * c:VW * (c + 1), lo:hi], v_s[:, j, g * GH + c, :], probs[:, n % PSLOTS, 0:hi - lo],
                              start=(j == 0), stop=(j == NT - 1), skip_group_check=True)
                last.then_inc(s_pv, 1)

            def outputs(i, a, g):
                pe.wait_ge(s_oc, i * N_OC + a * NGR + g + 1)
                last_rows = min(g + 1, NGR - 1)
                pe.wait_ge(s_mc, i * N_MC + a * NGR + last_rows + 1)
                if g == NGR - 1:
                    pe.wait_ge(s_on, i * N_ON + a * NGR + g)
                for t in range(NT):
                    last = nc.tensor.transpose(dn[:, t * P:(t + 1) * P], o_t[:, t * P:(t + 1) * P], ident[:, :])
                last.then_inc(s_op, 1)

            def hidden(f, n):
                u, m = n // NH, n % NH
                if n == 0:
                    pe.wait_ge(s_gr, f + 1)
                else:
                    pe.wait_ge(s_ht, f * N_HT + n)
                for half in range(2):
                    for c in range(NC):
                        col = half * HID + m * P
                        last = mm(fb[half][:, :], wup_s[:, u, c, col:col + P], xn_t[:, c, :],
                                  start=(c == 0), stop=(c == NC - 1))
                last.then_inc(s_up, 1)

            def expert_out(f, q):
                if q < 2:
                    pe.wait_ge(s_ht, f * N_HT + 2 * NH)
                else:
                    pe.wait_ge(s_er, f * N_ER + q - 1)
                t, k = (q, None) if q < NT else divmod(q - NT, NE // 2)
                for m in range(NH):
                    rows = slice(t * P, (t + 1) * P)
                    if k is None:
                        last = mm(fb[q % 2][:, 0:E], h_t[:, 0, m, rows], wso_s[:, m, :], start=(m == 0), stop=(m == NH - 1))
                    else:
                        last = mm(fb[q % 2][:, :], h_t[:, 1, m, rows],
                                  w2_s[:, m, 2 * k:2 * k + 2, :].rearrange("p e n -> p (e n)"),
                                  start=(m == 0), stop=(m == NH - 1))
                last.then_inc(s_eo, 1)

            def experts_begin(f, e):
                pe.wait_ge(s_x2, f + 1)
                if e is not None:
                    pe.wait_ge(s_er, (e + 1) * N_ER)
                transpose_rows(x2, fb, s_fp)
                pe.wait_ge(s_fc, (f + 1) * N_FC)
                for t in range(NT):
                    last = project_rows(fb[0][:, t * 16:t * 16 + NG + NE], wgate_s, xn_t, t)
                last.then_inc(s_gl, 1)

            def attention(i, f, a):
                pe.wait_ge(s_sa, i * N_SA + (a + 1) * 8)
                pe.wait_ge(s_sd, i * N_SD + (a + 1) * 8)
                for m in range(-LEAD, ALL):
                    if m + LEAD < ALL:
                        max_unit(i, a, *divmod(m + LEAD, UNITS))
                    if m >= 0:
                        g, n = divmod(m, UNITS)
                        if n == 0 and g >= 1:
                            weigh(i, a, g - 1, NT - 1)
                        score_unit(i, a, g, n)
                        if n % GH == 2 and n > GH:
                            weigh(i, a, g, n // GH - 1)
                        if n == 4 and g >= 1:
                            outputs(i, a, g - 1)
                    if (m + LEAD) % UNITS == ROWS_AT and UNITS < m + LEAD < ALL + UNITS:
                        max_rows(i, a, (m + LEAD) // UNITS - 1)
                    if f is not None and a == 0 and m in HIDDEN_AT:
                        hidden(f, HIDDEN_AT[m])
                    if f is not None and a == 1 and m in OUT_AT:
                        expert_out(f, OUT_AT[m])
                weigh(i, a, NGR - 1, NT - 1)
                outputs(i, a, NGR - 1)

            def project_attention(i, a, w):
                pe.wait_ge(s_on, i * N_ON + (a + 1) * NGR)
                transpose_rows(o_s, pair, s_tp)
                pe.wait_ge(s_tc, i * N_TC + (2 + 2 * a) * NC)
                for m in range(2):
                    for t in (2 * m, 2 * m + 1):
                        last = project_rows(st[m][:, (t % 2) * E:(t % 2 + 1) * E], w, xn_t, t)
                    last.then_inc(s_pj, 1)

            def heads(i, a, f, outs):
                for t in range(NT):
                    if f is not None and t < len(outs):
                        expert_out(f, outs[t])
                    if t >= 2:
                        pe.wait_ge(s_rp, i * N_RP + a * NT + t - 1)
                    if a == 0:
                        project_rows(pair[t % 2][:, :], win_t[:, :, 0:2 * E], xn_t, t).then_inc(s_qk, 1)
                    else:
                        project_rows(pair[t % 2][:, 0:E], wq_s, xn_t, t)
                        mm(pair[t % 2][:, E:2 * E], c_t[0:DC, t * P:(t + 1) * P], wkv_s[0:DC, :],
                           start=True, stop=True).then_inc(s_qk, 1)
                    if t >= 1:
                        pe.wait_ge(s_vc, i * N_VC + a * NT + t)
                    if a == 0:
                        project_rows(vb[:, 0:E], win_t[:, :, 2 * E:3 * E], xn_t, t).then_inc(s_v, 1)
                    else:
                        mm(vb[:, 0:E], c_t[DC:2 * DC, t * P:(t + 1) * P], wkv_s[DC:2 * DC, :],
                           start=True, stop=True).then_inc(s_v, 1)
                    if t >= 1:
                        stacks(i, a, t - 1)
                if f is not None:
                    for q in outs[NT:]:
                        expert_out(f, q)
                stacks(i, a, NT - 1)

            def batch(i, f, e):
                pe.wait_ge(s_xa, i + 1)
                transpose_rows(xa, pair, s_tp)
                pe.wait_ge(s_tc, i * N_TC + NC)
                if f is not None:
                    pe.wait_ge(s_pr, i * N_PR)
                heads(i, 0, e, OUT_LAST)
                if f is not None:
                    experts_begin(f, e)
                attention(i, f, 0)
                project_attention(i, 0, wout_t)
                if f is not None:
                    for q in OUT_FIRST:
                        expert_out(f, q)
                pe.wait_ge(s_xn, i + 1)
                transpose_rows(xn, pair, s_tp)
                pe.wait_ge(s_tc, i * N_TC + 3 * NC)
                for c in range(NC):
                    last = mm(st[0][:, :], wc_s[:, c, :], xn_t[:, c, :], start=(c == 0), stop=(c == NC - 1))
                last.then_inc(s_c, 1)
                pe.wait_ge(s_cc, i + 1)
                heads(i, 1, f, OUT_SECOND)
                attention(i, f, 1)
                project_attention(i, 1, wo_s)

            pe.wait_ge(s_const, 5)
            pe.wait_ge(s_w, 16 * N_LOADS)
            for r in range(8):
                if r >= 3:
                    pe.wait_ge(s_wc, r - 2)
                for c in range(NC):
                    last = nc.tensor.transpose(tri[r % 3][:, c * P:(c + 1) * P], w_raw[:, r, c * P:(c + 1) * P], ident[:, :])
                last.then_inc(s_wt, 1)
            pe.wait_ge(s_wc, 8)
            batch(0, None, None)
            batch(1, 0, None)
            with pe.Fori(2, B) as i:
                batch(i, i - 1, i - 2)
            for q in OUT_LAST:
                expert_out(B - 2, q)
            experts_begin(B - 1, B - 2)
            for n in range(2 * NH):
                hidden(B - 1, n)
            for q in range(OUTS):
                expert_out(B - 1, q)

        @block.vector
        def _(dve):
            v = nc.vector
            steps = [0]

            def done(ins):
                ins.then_inc(s_dve, 1)
                steps[0] += 1
                dve.wait_ge(s_dve, steps[0])

            def count_anew():
                dve.sem_clear(s_dve)
                steps[0] = 0

            def moments(rows):
                for t in range(NT):
                    last = v.bn_stats(stats[:, t, :], rows(t))
                done(last)
                for t in range(NT):
                    last = v.bn_aggr(mv[:, t, :], stats[:, t, :])
                done(last)

            def inverse_root():
                done(v.tensor_scalar(bits[:, :], var[:, :].bitcast(I32), 1, None, ALU.logical_shift_right))
                done(v.tensor_scalar(rstd[:, :].bitcast(I32), bits[:, :], -1.0, RSQRT_MAGIC, ALU.mult, ALU.add))
                for _ in range(3):
                    done(v.tensor_tensor(nt1[:, :], rstd[:, :], rstd[:, :], ALU.mult))
                    done(v.scalar_tensor_tensor(nt2[:, :], nt1[:, :], -0.5, var[:, :], ALU.mult, ALU.mult))
                    done(v.scalar_tensor_tensor(rstd[:, :], nt2[:, :], 1.5, rstd[:, :], ALU.add, ALU.mult))

            def layer_scale():
                done(v.tensor_scalar(var[:, :], mv[:, :, 1], LN_EPS, None, ALU.add))
                inverse_root()

            def rms_scale():
                done(v.tensor_tensor(nt1[:, :], mv[:, :, 0], mv[:, :, 0], ALU.mult))
                done(v.scalar_tensor_tensor(var[:, :], nt1[:, :], RMS_EPS, mv[:, :, 1], ALU.add, ALU.add))
                inverse_root()

            def centred(dst, rows):
                for t in range(NT):
                    last = v.tensor_scalar(dst(t), rows(t), mv[:, t, 0:1], rstd[:, t:t + 1], ALU.subtract, ALU.mult)
                return last

            def rope_products(i, a, t):
                bf, n = t % 2, a * NT + t
                dve.wait_ge(s_qk, i * N_QK + n + 1)
                if t >= 2:
                    dve.wait_ge(s_lo, i * N_LO + n - 1)
                if t >= 1:
                    dve.wait_ge(s_rot, i * N_ROT + n)
                src = pair[t % 2][:, :].rearrange("p (h d) -> p h d", d=D)
                pairs = pair[t % 2][:, :].rearrange("p (h f o) -> p h f o", f=D // 2, o=2)
                cross = rot_b[:, :, :].rearrange("p h (f o) -> p h f o", o=2)
                sin = rope_sin[:, a, t].rearrange("p (o f) -> p o f", o=2)
                v.tensor_tensor(rot[:, bf], src, rope_cos[:, a, t:t + 1, :].to_broadcast([P, 2 * H, D]), ALU.mult)
                for o in range(2):
                    last = v.tensor_tensor(cross[:, :, :, o], pairs[:, :, :, 1 - o],
                                           sin[:, o:o + 1, :].to_broadcast([P, 2 * H, D // 2]), ALU.mult)
                last.then_inc(s_rp, 1)

            def copy_stacks(i, a, t):
                for k, dst in ((1, q_t), (3, k_t)):
                    dve.wait_ge(s_sp, i * N_SP + a * 16 + 4 * t + k + 1)
                    v.tensor_copy(dst[:, 4:8, t * P:(t + 1) * P],
                                  tri[(4 * t + k) % 3][:, :].rearrange("p (b q) -> p b q", b=4)).then_inc(s_sd, 1)

            def take_max(i, a, g, n):
                u = (a * NGR + g) * UNITS + n
                lo, hi = kcols(n // GH, a)
                dve.wait_ge(s_sm, i * N_SM + u + 1)
                return v.tensor_reduce(negmax[:, g % 2, n // GH, n % GH:n % GH + 1], sm[n % 2][:, 0:hi - lo], AX.X,
                                       ALU.max, negate=True).then_inc(s_mx, 1)

            def split_max(i, a, g):
                dve.wait_ge(s_mx, i * N_MX + (a * NGR + g + 1) * UNITS)
                if g >= 2:
                    dve.wait_ge(s_mp, i * N_MP + a * NGR + g - 1)
                m = negmax[:, g % 2].rearrange("p t (b h) -> p t h b", b=2)
                hi = m_split[:, g % 2, :, :, 0, :]
                lo = m_split[:, g % 2, :, :, 1, :]
                done(v.tensor_copy(hi, m))
                v.tensor_tensor(lo, m, hi.bitcast(F32), ALU.subtract).then_inc(s_ms, 1)

            def normalise(i, a, g):
                dve.wait_ge(s_op, i * N_OP + a * NGR + g + 1)
                o = dn[:, :].rearrange("p (t h w) -> p t h w", t=NT, h=GH)
                done(v.reciprocal(den[:, :, :], o[:, :, :, D]))
                for t in range(NT):
                    last = v.tensor_tensor(
                        o_s[:, t, g * GH * D:(g + 1) * GH * D].rearrange("p (h d) -> p h d", h=GH), o[:, t, :, 0:D],
                        den[:, t].rearrange("p (h o) -> p h o", o=1).to_broadcast([P, GH, D]), ALU.mult)
                last.then_inc(s_on, 1)


            def heads(i, a, beside):
                rope_products(i, a, 0)
                for t in range(NT):
                    if t + 1 < NT:
                        rope_products(i, a, t + 1)
                    beside(t)
                    copy_stacks(i, a, t)

            def attention(i, f, e, a, more):
                for m in range(-LEAD, ALL):
                    if m + LEAD < ALL:
                        take_max(i, a, *divmod(m + LEAD, UNITS))
                    if (m + LEAD) % UNITS == UNITS - 1 and m + LEAD < ALL:
                        split_max(i, a, (m + LEAD) // UNITS)
                    if m >= UNITS and m % UNITS == 6:
                        normalise(i, a, m // UNITS - 1)
                    if f is not None and a == 0 and m - DVE_LAG in HIDDEN_AT:
                        hidden(f, HIDDEN_AT[m - DVE_LAG])
                    if f is not None and a == 1 and m - DVE_LAG in OUT_AT:
                        expert_out(f, OUT_AT[m - DVE_LAG])
                    if e is not None and a == 0 and m in FINISH_AT:
                        finish(e, FINISH_AT[m])
                    if a == 1 and more and m in SOURCE_AT:
                        first_source(i + 1, SOURCE_AT[m])
                normalise(i, a, NGR - 1)

            def projected(t):
                return st[t // 2][:, (t % 2) * E:(t % 2 + 1) * E]

            def first_source(i, part):
                if part == 0:
                    dve.wait_ge(s_x, i * 16 + 16)
                    moments(lambda t: x_s[:, t, :])
                else:
                    layer_scale()
                    centred(lambda t: xa[:, t, :], lambda t: x_s[:, t, :]).then_inc(s_xa, 1)

            def gates(i):
                dve.wait_ge(s_gl, i + 1)
                lg = fb[0][:, 0:NT * 16].rearrange("p (t n) -> p t n", t=NT)[:, :, 0:NG + NE]
                v.tensor_tensor(logit[:, :, :], lg,
                                bias_s[:, :].rearrange("p (o n) -> p o n", o=1).to_broadcast([P, NT, NG + NE]),
                                ALU.add).then_inc(s_gr, 1)
                dve.wait_ge(s_gr, i + 1)
                v.tensor_tensor(ediff[:, :, :], logit[:, :, NG + EPG:NG + NE], logit[:, :, NG:NG + EPG], ALU.subtract)
                done(v.tensor_tensor(gd[:, :], logit[:, :, 1], logit[:, :, 0], ALU.subtract))
                v.tensor_scalar(gsel[:, :], gd[:, :], 0.0, None, ALU.is_gt)
                done(v.tensor_scalar(nt1[:, :], gd[:, :], -1.0, None, ALU.mult))
                sel = gsel[:, :].rearrange("p (t o) -> p t o", o=1).to_broadcast([P, NT, EPG])
                done(v.tensor_copy(esel[:, :, :], logit[:, :, NG:NG + EPG]))
                done(v.tensor_copy(ediff[:, :, :], sel))
                v.tensor_tensor(gabs[:, :], gd[:, :], nt1[:, :], ALU.min).then_inc(s_ge, 1)
                done(v.copy_predicated(esel[:, :, :], ediff[:, :, :].bitcast(I32), logit[:, :, NG + EPG:NG + NE]))
                done(v.tensor_reduce(emax[:, :], esel[:, :, :], AX.X, ALU.max))
                v.tensor_tensor(esub[:, :, :], esel[:, :, :],
                                emax[:, :].rearrange("p (t o) -> p t o", o=1).to_broadcast([P, NT, EPG]),
                                ALU.subtract).then_inc(s_ge, 1)
                for t in range(NT):
                    one = esel[:, t].rearrange("p (e o) -> p e o", o=1).to_broadcast([P, EPG, EPG])
                    other = esel[:, t:t + 1, :].to_broadcast([P, EPG, EPG])
                    v.tensor_tensor(egt[:, t], other, one, ALU.is_gt)
                    last = v.tensor_tensor(eeq[:, t], other, one, ALU.is_equal)
                done(last)
                for t in range(NT):
                    last = v.tensor_tensor(eeq[:, t], eeq[:, t], lower[:, :, :], ALU.mult)
                done(last)
                done(v.tensor_tensor(egt[:, :, :, :], egt[:, :, :, :], eeq[:, :, :, :], ALU.add))
                done(v.tensor_reduce(rank[:, :, :], egt[:, :, :, :], AX.X, ALU.add))
                dve.wait_ge(s_gx, i * N_GX + 2)
                done(v.tensor_scalar(gprob[:, :], gexp[:, :], 1.0, None, ALU.add))
                done(v.tensor_reduce(esum[:, :], eexp[:, :, :], AX.X, ALU.add))
                done(v.tensor_tensor(gprob[:, :], gprob[:, :], esum[:, :], ALU.mult))
                done(v.reciprocal(gprob[:, :], gprob[:, :]))
                done(v.scalar_tensor_tensor(ew[:, :, :], rank[:, :, :], 2.0, eexp[:, :, :], ALU.is_lt, ALU.mult))
                done(v.tensor_tensor(ew[:, :, :], ew[:, :, :],
                                     gprob[:, :].rearrange("p (t o) -> p t o", o=1).to_broadcast([P, NT, EPG]), ALU.mult))
                done(v.tensor_tensor(gate[:, :, EPG:NE], ew[:, :, :], sel, ALU.mult))
                done(v.tensor_tensor(gate[:, :, 0:EPG], ew[:, :, :], gate[:, :, EPG:NE], ALU.subtract))


            def hidden(f, n):
                dve.wait_ge(s_th, f * N_TH + n + 1)
                v.scalar_tensor_tensor(sg[:, :], th[:, :], 1.0, fb[0][:, :], ALU.add,
                                       ALU.mult).then_inc(s_sg, 1)
                dve.wait_ge(s_sg, f * N_SG + n + 1)
                v.scalar_tensor_tensor(h_t[:, n // NH, n % NH, :], sg[:, :], 0.5, fb[1][:, :], ALU.mult,
                                       ALU.mult).then_inc(s_ht, 1)

            def expert_out(f, q):
                dve.wait_ge(s_eo, f * N_EO + q + 1)
                if q < NT:
                    if q == 0:
                        dve.wait_ge(s_yfree, 16 * (f + 1))
                    v.tensor_tensor(acc[:, q, :], fb[q % 2][:, 0:E], x2[:, q, :], ALU.add).then_inc(s_er, 1)
                    return
                t, k = divmod(q - NT, NE // 2)
                dve.wait_ge(s_er, f * N_ER + q)
                for e in (2 * k, 2 * k + 1):
                    add = v.scalar_tensor_tensor(acc[:, t, :], fb[q % 2][:, (e % 2) * E:(e % 2 + 1) * E],
                                                 gate[:, t, e:e + 1], acc[:, t, :], ALU.mult, ALU.add)
                    if e % 2 == 0:
                        done(add)
                add.then_inc(s_er, 1)

            def weighted(dst, src, norm):
                for t in range(NT):
                    last = v.scalar_tensor_tensor(dst[:, t, :], src[:, t, :], rstd[:, t:t + 1], norm_w[:, norm, :],
                                                  ALU.mult, ALU.mult)
                return last

            def finish(f, part):
                if part == 0:
                    dve.wait_ge(s_er, (f + 1) * N_ER)
                    moments(lambda t: acc[:, t, :])
                    rms_scale()
                elif part == 1:
                    done(weighted(acc, acc, 1))
                    moments(lambda t: acc[:, t, :])
                elif part == 2:
                    layer_scale()
                else:
                    done(centred(lambda t: acc[:, t, :], lambda t: acc[:, t, :]))
                    dve.wait_ge(s_xk, 16 * (f + 1))
                    v.tensor_tensor(acc[:, :, :], acc[:, :, :], x1_kept[:, :, :], ALU.add).then_inc(s_y, 1)
                    dve.wait_ge(s_y, f + 1)
                    v.memset(spare[:, :], 0.0).then_inc(s_xf, 1)

            def expert_source(f, part):
                if part == 0:
                    moments(lambda t: x2[:, t, :])
                elif part == 1:
                    rms_scale()
                elif part == 2:
                    weighted(x2, x2, 0).then_inc(s_x2, 1)

            def out_now(f, outs):
                if f is not None:
                    for q in outs:
                        expert_out(f, q)

            def batch(i, f, e, more):
                def beside_first(t):
                    out_now(e, OUT_LAST[t:t + 1])
                    if f is not None:
                        expert_source(f, t)

                def beside_second(t):
                    out_now(f, OUT_SECOND[t:t + 1])

                heads(i, 0, beside_first)
                out_now(e, OUT_LAST[NT:])
                if f is not None:
                    gates(f)
                attention(i, f, e, 0, more)
                dve.wait_ge(s_pj, i * N_PJ + 2)
                moments(projected)
                out_now(f, OUT_FIRST[0:1])
                layer_scale()
                out_now(f, OUT_FIRST[1:2])
                if f is not None:
                    dve.wait_ge(s_xk, 16 * (f + 1))
                done(centred(lambda t: x1[:, t, :], projected))
                v.tensor_tensor(x1[:, :, :], x_s[:, :, :], x1[:, :, :], ALU.add).then_inc(s_res, 1)
                dve.wait_ge(s_res, i + 1)
                v.memset(spare[:, :], 0.0).then_inc(s_pr, 1)
                out_now(f, OUT_FIRST[2:3])
                moments(lambda t: x1[:, t, :])
                out_now(f, OUT_FIRST[3:4])
                layer_scale()
                centred(lambda t: xn[:, t, :], lambda t: x1[:, t, :]).then_inc(s_xn, 1)
                out_now(f, OUT_FIRST[4:])
                heads(i, 1, beside_second)
                attention(i, f, e, 1, more)
                dve.wait_ge(s_pj, i * N_PJ + 4)
                for t in range(NT):
                    last = v.tensor_tensor(x2[:, t, :], projected(t), xn[:, t, :], ALU.add)
                last.then_inc(s_pr, 1)
                dve.wait_ge(s_pr, (i + 1) * N_PR)

            v.memset(v_s[:, :, :, :], 0.0)
            done(v.memset(stack[:, :, :, :].bitcast(F32), 0.0))
            v.memset(v_s[:, :, :, D:D + 1], 1.0).then_inc(s_fill, 1)
            v.memset(stack[:, :, H:2 * H, MROW:MROW + 2].bitcast(F32), 1.0).then_inc(s_fill, 1)
            v.memset(spare[:, :], 0.0).then_inc(s_xf, 1)
            dve.wait_ge(s_xf, 1)
            v.memset(spare[:, :], 0.0).then_inc(s_yfree, 16)
            dve.wait_ge(s_yfree, 16)
            dve.wait_ge(s_w, 16 * N_LOADS)
            dve.wait_ge(s_const, 5)
            first_source(0, 0)
            first_source(0, 1)
            batch(0, None, None, True)
            batch(1, 0, None, True)
            with dve.Fori(2, B - 1) as i:
                count_anew()
                batch(i, i - 1, i - 2, True)
            count_anew()
            batch(B - 1, B - 2, B - 3, False)
            out_now(B - 2, OUT_LAST)
            for part in range(4):
                finish(B - 2, part)
            for part in range(3):
                expert_source(B - 1, part)
            gates(B - 1)
            for n in range(2 * NH):
                hidden(B - 1, n)
            out_now(B - 1, range(OUTS))
            for part in range(4):
                finish(B - 1, part)


def rope_tables():
    ts = np.arange(T, dtype=np.float32)[:, None]
    ds = np.arange(D // 2, dtype=np.float32)
    out = np.zeros((2, 2, T, D), np.float32)
    for a, freqs in enumerate((np.exp(ds * np.float32(-np.log(10000.0) * 2.0 / D)),
                               np.float32(1.0) / np.float32(10000.0) ** (np.arange(0, D, 2, dtype=np.float32) / D))):
        angle = ts * freqs.astype(np.float32)[None, :]
        out[a, 0] = np.repeat(np.cos(angle), 2, axis=1)
        out[a, 1] = np.concatenate([-np.sin(angle), np.sin(angle)], axis=1)
    return np.ascontiguousarray(out.reshape(2, 2, NT, P, D).transpose(1, 3, 0, 2, 4))


_INS = ["L0_attn_query", "L0_attn_in_proj_w", "L0_attn_out_proj_w", "L0_ffn_Wq", "L0_ffn_Wk_c", "L0_ffn_Wv_c",
        "L0_ffn_Wk", "L0_ffn_Wv", "L0_ffn_Wo", "L0_ffn_W_shared_in", "L0_ffn_W_shared_out", "L0_ffn_W1_shared",
        "L0_ffn_W2_experts", "L0_ffn_Wg_gate", "L0_ffn_We_gate", "L0_ffn_group_bias", "L0_ffn_expert_bias",
        "L0_ffn_norm1_w", "L0_ffn_norm2_w"]


def kernel(**inputs):
    import concourse.bacc as bacc
    from concourse.bass_utils import run_bass_kernel_spmd

    nc = bacc.Bacc("TRN2", target_bir_lowering=False, num_devices=1)
    arrays = {f"in_{n}": np.ascontiguousarray(inputs[n]) for n in _INS}
    arrays["in_rope"] = rope_tables()
    args = [nc.dram_tensor(n, a.shape, mybir.dt.from_np(a.dtype), kind="ExternalInput").ap() for n, a in arrays.items()]
    out = nc.dram_tensor("out_0", (B, T, E), F32, kind="ExternalOutput").ap()
    build(nc, *args, out)
    r = run_bass_kernel_spmd(nc, [arrays], core_ids=[0])
    return r.results[0]["out_0"]
```

```python
import numpy as np
import concourse.bass as bass
from concourse import mybir
from contextlib import ExitStack

F32 = mybir.dt.float32
F32R = mybir.dt.float32r
BF16 = mybir.dt.bfloat16
I32 = mybir.dt.int32
ALU = mybir.AluOpType
ACT = mybir.ActivationFunctionType
AX = mybir.AxisListType

P = 128
B, T, E = 8, 512, 256
H, D = 16, 16
NT = T // P
NC = E // P
CONTEXT = 250
BACK = 3
DC = E // 4
HID = 512
NH = HID // P
NG, NE, EPG = 2, 8, 4
LN_EPS, RMS_EPS = 1e-5, 1e-6
SK = 64
MROW = 3 * D
GH = 4
NGR = H // GH
UNITS = GH * NT
PSLOTS = 8
VW = 32
MASKED = -1e38
PAIRS = NE // 2
OUTS = NT + NT * PAIRS
LEAD = 28
ALL = NGR * UNITS
def spread(steps, first, last):
    return [first + s * (last - first) // (steps - 1) for s in range(steps)]


LAST_STACKS_AT = 6 - LEAD
ROWS_FROM, LOGITS_AT = 2 - LEAD, 7 - LEAD
QUIET = [g * UNITS + n for g in range(NGR) for n in (2, 5, 8, 12)]
QUIET_OUT = [g * UNITS + n for g in range(NGR) for n in (2, 8, 12)]
HIDDEN_AT = spread(8 * NH - len(QUIET), 10 - LEAD, -1) + QUIET
OUT_FIRST, OUT_BESIDE = range(2, 7), range(9, 16)
OUT_END = {0: (((0, 0), (0, 1)), ((0, 2), (0, 3)), ((1, 0), (1, 1), (1, 2), (1, 3))),
           1: (((16, 0), (16, 1)), ((16, 2), (16, 3)), ())}
OUT_HEADS = {0: ((17,), (), (18,), (19,), ()), 1: ((), (7,), (), (8,), ())}
OUT_AT = spread(len(OUT_BESIDE) * NH - len(QUIET_OUT), 1 - LEAD, -1) + QUIET_OUT
ACT_LAG, DVE_LAG, HIGH_LAG = 1, 2, 3
GATES_FROM = LOGITS_AT + 2
GATE_EXPS_AT = (GATES_FROM + 6, GATES_FROM + 12)
SOURCE_STEPS = 8
STEPS_AT_LAST = 9
SOURCE_FROM = 36
LEAD_WIDE, TAIL_WIDE = range(3 * GH, LEAD - GH), ALL - LEAD + 4
ROWS_AT = 2
RSQRT_MAGIC = float(0x5F3759DF)


def build(nc, x, in_w, out_w, wq, wkc, wvc, wk, wv, wo, w_si, w_so, w1, w2, wgg, weg,
          g_bias, e_bias, n1w, n2w, rope, out):
    ctx = ExitStack()
    with ctx:
        def sb(name, shape, dt=F32):
            return ctx.enter_context(nc.sbuf_tensor(name, shape, dt))

        def sem(name):
            return ctx.enter_context(nc.semaphore(name))

        ident = sb("ident", [P, P])
        identb = sb("identb", [P, P], BF16)
        mask_kq = sb("mask_kq", [P, BACK * P], BF16)
        mask_qk = sb("mask_qk", [P, BACK * P], BF16)
        lower = sb("lower", [P, EPG, EPG])
        rope_cos = sb("rope_cos", [P, 2, NT, D])
        rope_sin = sb("rope_sin", [P, 2, NT, D])
        win_t = sb("win_t", [P, NC, 3 * E])
        wout_t = sb("wout_t", [P, NC, E])
        wq_s = sb("wq_s", [P, NC, E])
        wc_s = sb("wc_s", [P, NC, 2 * DC])
        wkv_s = sb("wkv_s", [P, E])
        wo_s = sb("wo_s", [P, NC, E])
        wup_s = sb("wup_s", [P, 2, NC, 2 * HID])
        wso_s = sb("wso_s", [P, NH, E])
        w2_r = sb("w2_r", [P, 2, 2, NH, 2 * E], F32R)
        wgate_s = sb("wgate_s", [P, NC, NG + NE])
        bias_s = sb("bias_s", [P, NG + NE])
        norm_w = sb("norm_w", [P, 2, E])

        x_s = sb("x_s", [P, NT, E])
        xa = sb("xa", [P, NT, E])
        x1_back = xa
        xn_t = sb("xn_t", [P, NC, T])
        rot = sb("rot", [P, 2, 2 * H, D])
        rot_b = sb("rot_b", [P, 2 * H, D])
        stack = sb("stack", [P, 2, 2 * H, SK], F32R)
        q_t = sb("q_t", [P, H // 2, T], F32R)
        k_t = sb("k_t", [P, H // 2, T], F32R)
        v_s = sb("v_s", [P, NT, H, VW])
        negmax = sb("negmax", [P, 2, NT, GH])
        m_split = sb("m_split", [P, 2, NT, 2, 2, 2], F32R)
        m_t = rot_b[0:8].rearrange("p h d -> p (h d)")
        probs = sb("probs", [P, PSLOTS, T])
        w_raw = probs[:, 0:4, :].rearrange("p s (r e) -> p (s r) e", e=E)
        o_t = sb("o_t", [P, T])
        den = sb("den", [P, NT, GH])
        o_s = sb("o_s", [P, NT, E])
        x1 = o_s
        x2 = sb("x2", [P, NT, E])
        xn = x2
        th = sb("th", [P, T])
        c_t = th
        sg = sb("sg", [P, 2, T])
        h_s = sb("h_s", [P, NH, T])
        h_r = sb("h_r", [P, 2, NH, T], F32R)
        acc = sb("acc", [P, NT, E])
        w2_raw = [h_s[:, :, 0:E], h_s[:, :, E:2 * E]]
        stats = sb("stats", [P, NT, 6])
        mv = sb("mv", [P, NT, 2])
        spare = sb("spare", [P, 1])
        var = sb("var", [P, NT])
        bits = sb("bits", [P, NT], I32)
        rstd = sb("rstd", [P, NT])
        nt1 = sb("nt1", [P, NT])
        nt2 = sb("nt2", [P, NT])
        logit = sb("logit", [P, NT, NG + NE])
        gd = sb("gd", [P, NT])
        gsel = sb("gsel", [P, NT])
        gabs = sb("gabs", [P, NT])
        gexp = sb("gexp", [P, NT])
        gprob = sb("gprob", [P, NT])
        ediff = sb("ediff", [P, NT, EPG])
        esel = sb("esel", [P, NT, EPG])
        emax = sb("emax", [P, NT])
        esub = sb("esub", [P, NT, EPG])
        eexp = sb("eexp", [P, NT, EPG])
        esum = sb("esum", [P, NT])
        egt = sb("egt", [P, NT, EPG, EPG])
        eeq = sb("eeq", [P, NT, EPG, EPG])
        rank = sb("rank", [P, NT, EPG])
        ew = sb("ew", [P, NT, EPG])
        gate = sb("gate", [P, NT, NE])

        def bank(name):
            return ctx.enter_context(nc.psum_tensor(name, [P, T], F32))

        st = [bank("st0"), bank("st1")]
        sm = [bank("sm0"), bank("sm1")]
        ot = bank("ot")
        dn = bank("dn")
        fb = [bank("fb0"), bank("fb1")]
        pair = [dn, ot]
        tri = [st[0], st[1], sm[0]]
        vb = sm[1]

        s_w1 = sem("first_projection_weights_loaded")
        s_w = sem("weights_loaded")
        s_x = sem("x_loaded")
        s_const = sem("constants_made")
        s_wt = sem("weight_transposes_done")
        s_wc = sem("weight_transposes_copied")
        s_fill = sem("fixed_columns_filled")
        s_dve = sem("vector_step_done")
        s_pool = sem("pool_step_done")
        s_xa = sem("first_source_ready")
        s_xn = sem("second_source_ready")
        s_x2 = sem("expert_source_ready")
        s_tp, N_TP = sem("row_transposes_done"), 4 * NC
        s_tc, N_TC = sem("row_transposes_copied"), 4 * NC
        s_fp, N_FP = sem("expert_rows_transposed"), NC
        s_fc, N_FC = sem("expert_rows_copied"), NC
        s_qk, N_QK = sem("qk_projected"), 2 * NT
        s_v, N_V = sem("v_projected"), 2 * NT
        s_vc, N_VC = sem("v_copied"), 2 * NT
        s_c, s_cc = sem("compressed_projected"), sem("compressed_copied")
        s_rp, N_RP = sem("rope_products_ready"), 2 * NT
        s_rot, N_ROT = sem("rotated_ready"), 2 * NT
        s_hi, N_HI = sem("high_parts_ready"), 2 * NT
        s_lo, N_LO = sem("low_parts_ready"), 2 * NT
        s_sp, N_SP = sem("stack_transposes_done"), 8 * NT
        s_sa, N_SA = sem("stacks_copied_by_act"), 4 * NT
        s_sd, N_SD = sem("stacks_copied_by_dve"), 4 * NT
        s_sm, N_SM = sem("max_scores_done"), 2 * NGR * UNITS
        s_mx, N_MX = sem("max_taken"), 2 * NGR * UNITS
        s_ms, N_MS = sem("max_split"), 2 * NGR
        s_mp, N_MP = sem("max_transposed"), 2 * NGR
        s_mc, N_MC = sem("max_rows_copied"), 2 * NGR
        s_mr, N_MR = [sem("max_rows_placed0"), sem("max_rows_placed1")], 2 * 64 * NGR // 2
        s_st, N_ST = sem("scores_done"), 2 * NGR * UNITS
        s_ex, N_EX = sem("exps_done"), 2 * NGR * UNITS
        s_pv, N_PV = sem("values_weighed"), 2 * NGR * NT
        s_oc, N_OC = sem("outputs_copied"), 2 * NGR
        s_op, N_OP = sem("outputs_transposed"), 2 * NGR
        s_on, N_ON = sem("outputs_normalised"), 2 * NGR
        s_pj, N_PJ = sem("attention_projected"), 4
        s_pr, N_PR = sem("projection_read"), 2
        s_res = sem("first_residual_added")
        s_ctr, s_ctd = sem("centring_ready"), sem("rows_centred")
        s_gl, s_gr = sem("gate_logits_done"), sem("gate_logits_read")
        s_ge, N_GE = sem("gate_exponents_ready"), 2
        s_gx, N_GX = sem("gate_exps_done"), 2
        s_up, N_UP = sem("gated_half_projected"), 2 * NH
        s_ub, N_UB = sem("other_half_projected"), 2 * NH
        s_th, N_TH = sem("tanh_ready"), 2 * NH
        s_sg, N_SG = sem("gated_half_done"), 2 * NH
        s_ht, N_HT = sem("hidden_ready"), 2 * NH
        s_eo, N_EO = sem("expert_out_done"), OUTS
        s_er, N_ER = sem("expert_out_read"), OUTS
        s_xk, s_xb = sem("x1_stored"), sem("x1_loaded_back")
        s_y = sem("y_ready")
        s_yfree = sem("y_stored_or_first_free")

        s_w2, N_W2 = [sem("expert_pair_loaded0"), sem("expert_pair_loaded1")], 16 * PAIRS // 2
        s_w2r = [sem("raw_expert_loaded0"), sem("raw_expert_loaded1")]
        s_w2h, s_w2l = sem("expert_weights_high_made"), sem("expert_weights_low_made")
        s_w2p = sem("expert_pair_stored")
        s_hh, N_HH = sem("hidden_high_made"), NH
        s_hl, N_HL = sem("hidden_low_made"), NH
        w2_parts = nc.dram_tensor("w2_parts", (PAIRS, P, 2, NH, 2 * E), F32, kind="Internal").ap()

        x1_kept = nc.dram_tensor("x1_kept", (B, P, NT, E), F32, kind="Internal").ap()

        x_v = x.rearrange("b (t p) e -> b p t e", p=P)
        out_v = out.rearrange("b (t p) e -> b p t e", p=P)

        def qcols(j, a):
            return (j * P, min(T, (j + BACK) * P)) if a == 0 else (0, T)

        def kcols(t, a):
            return (max(0, (t + 1 - BACK) * P), (t + 1) * P) if a == 0 else (0, T)

        def max_bank(u):
            return (sm + st)[u % 4] if u in LEAD_WIDE else sm[u % 2]

        def score_bank(u):
            return (st + sm)[u % 4] if u >= TAIL_WIDE else st[u % 2]

        def stack_bank(a, t, k):
            return ot if (a, t, k) == (0, NT - 1, 2) else tri[(4 * t + k) % 3]

        def projected(t):
            return st[t // 2][:, (t % 2) * E:(t % 2 + 1) * E]

        block = ctx.enter_context(nc.Block())


        @block.sync
        def _(sp):
            first_loads = [
                (w_raw[:, 0:6, :], in_w.rearrange("(r p) e -> p r e", p=P)),
                (w_raw[:, 6:8, :], out_w.rearrange("(r p) e -> p r e", p=P)),
                (rope_cos[:, :, :, :], rope[0]),
                (rope_sin[:, :, :, :], rope[1]),
            ]
            loads = [
                (wq_s[:, :, :], wq.rearrange("(c p) e -> p c e", p=P)),
                (wc_s[:, :, 0:DC], wkc.rearrange("(c p) e -> p c e", p=P)),
                (wc_s[:, :, DC:2 * DC], wvc.rearrange("(c p) e -> p c e", p=P)),
                (wkv_s[0:DC, :], wk),
                (wkv_s[DC:2 * DC, :], wv),
                (wo_s[:, :, :], wo.rearrange("(c p) e -> p c e", p=P)),
                (wgate_s[:, :, 0:NG], wgg.rearrange("(c p) e -> p c e", p=P)),
                (wgate_s[:, :, NG:NG + NE], weg.rearrange("(c p) e -> p c e", p=P)),
                (bias_s[:, 0:NG], g_bias.rearrange("(o n) -> o n", o=1).to_broadcast([P, NG])),
                (bias_s[:, NG:NG + NE], e_bias.rearrange("(o n) -> o n", o=1).to_broadcast([P, NE])),
                (norm_w[:, 0, :], n1w.rearrange("(o n) -> o n", o=1).to_broadcast([P, E])),
                (norm_w[:, 1, :], n2w.rearrange("(o n) -> o n", o=1).to_broadcast([P, E])),
                (wup_s[:, 0, :, :], w_si.rearrange("(c p) n -> p c n", p=P)),
                (wup_s[:, 1, :, :], w1.rearrange("(c p) n -> p c n", p=P)),
                (wso_s[:, :, :], w_so.rearrange("(c p) e -> p c e", p=P)),
            ]
            sp.dma_start(x_s[:, :, :], x_v[0]).then_inc(s_x, 16)
            for dst, src in first_loads:
                sp.dma_start(dst, src).then_inc(s_w1, 16)
            for dst, src in loads:
                sp.dma_start(dst, src).then_inc(s_w, 16)

            def place_maxima(i, a):
                for g in range(NGR):
                    sp.wait_ge(s_mc, i * N_MC + a * NGR + g + 1)
                    for half in range(2):
                        for part in range(2):
                            r, m = SK * half + MROW + part, 4 * half + 2 * part
                            sp.dma_start(q_t[r:r + 1, 2 * g:2 * g + 2, :].bitcast(F32),
                                         rot_b[m:m + 2].rearrange("p h d -> p (h d)")).then_inc(s_mr[g % 2], 16)

            def store(f):
                sp.wait_ge(s_y, f + 1)
                sp.dma_start(out_v[f], acc[:, :, :]).then_inc(s_yfree, 16)

            def x1_to_dram(i):
                sp.dma_start(x1_kept[i], x1[:, :, :]).then_inc(s_xk, 16)

            def x1_from_dram(e):
                sp.wait_ge(s_xk, 16 * (e + 1))
                sp.dma_start(x1_back[:, :, :], x1_kept[e]).then_inc(s_xb, 16)

            def load_pair(f, k, e):
                if k >= 2:
                    sp.wait_ge(s_eo, f * N_EO + NT + NT * (k - 1))
                elif e is not None:
                    sp.wait_ge(s_eo, e * N_EO + NT + NT * (k + PAIRS - 1))
                sp.dma_start(w2_r[:, k % 2].bitcast(F32), w2_parts[k]).then_inc(s_w2[k % 2], 16)

            def batch(i, f, e, more):
                if e is not None:
                    sp.wait_ge(s_tp, i * N_TP + NC)
                    x1_from_dram(e)
                place_maxima(i, 0)
                if f is not None:
                    load_pair(f, 0, e)
                    load_pair(f, 1, e)
                if e is not None:
                    store(e)
                sp.wait_ge(s_res, i + 1)
                x1_to_dram(i)
                if more:
                    sp.dma_start(x_s[:, :, :], x_v[i + 1]).then_inc(s_x, 16)
                if f is not None:
                    load_pair(f, 2, e)
                place_maxima(i, 1)
                if f is not None:
                    load_pair(f, 3, e)

            batch(0, None, None, True)
            sp.wait_ge(s_w2p, 16 * PAIRS)
            batch(1, 0, None, True)
            with sp.Fori(2, B - 1) as i:
                batch(i, i - 1, i - 2, True)
            batch(B - 1, B - 2, B - 3, False)
            load_pair(B - 1, 0, B - 2)
            load_pair(B - 1, 1, B - 2)
            x1_from_dram(B - 2)
            store(B - 2)
            load_pair(B - 1, 2, B - 2)
            load_pair(B - 1, 3, B - 2)
            x1_from_dram(B - 1)
            store(B - 1)
            sp.wait_ge(s_yfree, 16 * B + 16)

        N_FIRST_LOADS, N_LOADS = 4, 15

        @block.gpsimd
        def _(pool):
            g = nc.gpsimd
            g.memset(ident[:, :], 0.0).then_inc(s_pool, 1)
            g.memset(identb[:, :], 0.0).then_inc(s_pool, 1)
            g.memset(mask_kq[:, :], 0.0).then_inc(s_pool, 1)
            g.memset(mask_qk[:, :], 0.0).then_inc(s_pool, 1)
            g.memset(lower[:, :, :], 1.0).then_inc(s_pool, 1)
            pool.wait_ge(s_pool, 5)
            for m in (ident, identb):
                g.affine_select(out=m[:, :], in_=m[:, :], compare_op=ALU.not_equal, fill=1.0, base=0,
                                pattern=[[-1, P]], channel_multiplier=1).then_inc(s_const, 1)
            g.affine_select(out=mask_kq[:, :], in_=mask_kq[:, :], compare_op=ALU.is_ge, fill=MASKED, base=0,
                            pattern=[[1, BACK * P]], channel_multiplier=-1).then_inc(s_pool, 1)
            g.affine_select(out=mask_qk[:, :], in_=mask_qk[:, :], compare_op=ALU.is_ge, fill=MASKED,
                            base=(BACK - 1) * P, pattern=[[-1, BACK * P]], channel_multiplier=1).then_inc(s_pool, 1)
            pool.wait_ge(s_pool, 7)
            g.affine_select(out=mask_kq[:, :], in_=mask_kq[:, :], compare_op=ALU.is_ge, fill=MASKED,
                            base=CONTEXT - 1, pattern=[[-1, BACK * P]], channel_multiplier=1).then_inc(s_const, 1)
            g.affine_select(out=mask_qk[:, :], in_=mask_qk[:, :], compare_op=ALU.is_ge, fill=MASKED,
                            base=CONTEXT - 1 - (BACK - 1) * P, pattern=[[1, BACK * P]],
                            channel_multiplier=-1).then_inc(s_const, 1)
            g.affine_select(out=lower[:, :, :], in_=lower[:, :, :], compare_op=ALU.is_ge, fill=0.0, base=-1,
                            pattern=[[1, EPG], [-1, EPG]], channel_multiplier=0).then_inc(s_const, 1)

            def low_parts(i, a):
                for t in range(NT):
                    n, bf = a * NT + t, t % 2
                    pool.wait_ge(s_hi, i * N_HI + n + 1)
                    hi = stack[:, bf].bitcast(F32)
                    g.tensor_tensor(stack[:, bf, 0:H, 2 * D:3 * D], rot[:, bf, 0:H], hi[:, 0:H, 0:D], ALU.subtract)
                    g.tensor_tensor(stack[:, bf, H:2 * H, D:2 * D], rot[:, bf, H:2 * H], hi[:, H:2 * H, 0:D],
                                    ALU.subtract).then_inc(s_lo, 1)

            def load_raw(e):
                if e >= 2:
                    pool.wait_ge(s_w2l, e - 1)
                g.dma_start(w2_raw[e % 2], w2[e].rearrange("(c p) n -> p c n", p=P)).then_inc(s_w2r[e % 2], 16)

            def split_pair(k):
                if k >= 2:
                    pool.wait_ge(s_w2p, 16 * (k - 1))
                for e in (2 * k, 2 * k + 1):
                    hi, lo = (w2_r[:, k % 2, part, :, (e % 2) * E:(e % 2 + 1) * E] for part in range(2))
                    raw = w2_raw[e % 2]
                    pool.wait_ge(s_w2r[e % 2], 16 * (k + 1))
                    g.tensor_copy(hi, raw).then_inc(s_w2h, 1)
                    pool.wait_ge(s_w2h, e + 1)
                    g.tensor_tensor(lo, raw, hi.bitcast(F32), ALU.subtract).then_inc(s_w2l, 1)
                    if e + 2 < NE:
                        load_raw(e + 2)
                pool.wait_ge(s_w2l, 2 * k + 2)
                g.dma_start(w2_parts[k], w2_r[:, k % 2].bitcast(F32)).then_inc(s_w2p, 16)

            def hidden_low(f):
                for n in range(NH):
                    pool.wait_ge(s_hh, f * N_HH + n + 1)
                    g.tensor_tensor(h_r[:, 1, n, :], sg[:, n % 2, :], h_r[:, 0, n, :].bitcast(F32),
                                    ALU.subtract).then_inc(s_hl, 1)

            load_raw(0)
            load_raw(1)
            low_parts(0, 0)
            split_pair(0)
            split_pair(1)
            low_parts(0, 1)
            split_pair(2)
            split_pair(3)

            with pool.Fori(1, B) as i:
                low_parts(i, 0)
                hidden_low(i - 1)
                low_parts(i, 1)
            hidden_low(B - 1)

        @block.scalar
        def _(act):
            def copy(dst, src):
                return nc.scalar.activation(dst, src, ACT.Copy)

            def split_high(i, a):
                for t in range(NT):
                    n, bf = a * NT + t, t % 2
                    act.wait_ge(s_v, i * N_V + n + 1)
                    copy(v_s[:, t, :, 0:D], vb[:, 0:E].rearrange("p (h d) -> p h d", h=H)).then_inc(s_vc, 1)
                    act.wait_ge(s_rot, i * N_ROT + n + 1)
                    if t >= 2:
                        act.wait_ge(s_sp, i * N_SP + a * 16 + 4 * (t - 1))
                    for src, dst in ((rot[:, bf, 0:H], stack[:, bf, 0:H, 0:2 * D].rearrange("p h (r d) -> p h r d", r=2)),
                                     (rot[:, bf, H:2 * H],
                                      stack[:, bf, H:2 * H, :].rearrange("p h (r d) -> p h r d", r=2)[:, :, :, 0:D])):
                        last = copy(dst, src.rearrange("p h (o d) -> p h o d", o=1).to_broadcast([P, H, 2, D]))
                    last.then_inc(s_hi, 1)
                    if 1 <= t < NT - 1:
                        copy_stacks(i, a, t - 1)
                copy_stacks(i, a, NT - 2)
                if a == 1:
                    copy_stacks(i, a, NT - 1)

            def copy_stacks(i, a, t):
                for k, dst in ((0, q_t), (2, k_t)):
                    act.wait_ge(s_sp, i * N_SP + a * 16 + 4 * t + k + 1)
                    copy(dst[:, 0:4, t * P:(t + 1) * P],
                         stack_bank(a, t, k)[:, :].rearrange("p (b q) -> p b q", b=4)).then_inc(s_sa, 1)

            def copy_maxima(i, a, g):
                act.wait_ge(s_mp, i * N_MP + a * NGR + g + 1)
                copy(m_t, dn[0:8, :]).then_inc(s_mc, 1)

            def copy_outputs(i, a, g):
                act.wait_ge(s_pv, i * N_PV + (a * NGR + g + 1) * NT)
                copy(o_t[:, :], ot[:, :]).then_inc(s_oc, 1)

            def tanh(f, n):
                act.wait_ge(s_up, f * N_UP + n + 1)
                if n >= 1:
                    act.wait_ge(s_sg, f * N_SG + n)
                nc.scalar.activation(th[:, :], fb[0][:, :], ACT.Tanh, scale=0.5).then_inc(s_th, 1)

            def hidden_high(f, n):
                act.wait_ge(s_ht, f * N_HT + n + 1)
                copy(h_r[:, 0, n - NH, :], sg[:, n % 2, :]).then_inc(s_hh, 1)

            def gate_exp(f, k):
                act.wait_ge(s_ge, f * N_GE + k + 1)
                src, dst = ((gabs[:, :], gexp[:, :]), (esub[:, :, :], eexp[:, :, :]))[k]
                nc.scalar.activation(dst, src, ACT.Exp).then_inc(s_gx, 1)

            def attention(i, f, a):
                for m in range(-LEAD, ALL):
                    if a == 0 and m == LAST_STACKS_AT:
                        copy_stacks(i, a, NT - 1)
                    if m >= 0:
                        g, n = divmod(m, UNITS)
                        if n == 1 and g >= 1:
                            copy_outputs(i, a, g - 1)
                        u = a * ALL + m
                        lo, hi = qcols(n // GH, a)
                        act.wait_ge(s_st, i * N_ST + u + 1)
                        if m >= PSLOTS:
                            act.wait_ge(s_pv, i * N_PV + (u - PSLOTS) // GH + 1)
                        nc.scalar.activation(probs[:, n % PSLOTS, 0:hi - lo], score_bank(m)[:, 0:hi - lo], ACT.Exp,
                                             scale=float(D) ** -0.5).then_inc(s_ex, 1)
                    if (m + LEAD) % UNITS == ROWS_AT + ACT_LAG and UNITS < m + LEAD < ALL + UNITS:
                        copy_maxima(i, a, (m + LEAD) // UNITS - 1)
                    if f is not None and a == 0:
                        if m == ROWS_FROM:
                            copy_expert_rows(f)
                        if m in GATE_EXPS_AT:
                            gate_exp(f, GATE_EXPS_AT.index(m))
                        for n in range(2 * NH):
                            if HIDDEN_AT[4 * n + 1] + ACT_LAG == m:
                                tanh(f, n)
                            if n >= NH and min(HIDDEN_AT[4 * n + 3] + HIGH_LAG, ALL - 1) == m:
                                hidden_high(f, n)
                copy_outputs(i, a, NGR - 1)

            def copy_rows(i, n):
                for c in range(NC):
                    act.wait_ge(s_tp, i * N_TP + n * NC + c + 1)
                    copy(xn_t[:, c, :], pair[c][:, :]).then_inc(s_tc, 1)

            def centre(i):
                act.wait_ge(s_ctr, i + 1)
                for t in range(NT):
                    nc.scalar.activation(x1[:, t, :], projected(t), ACT.Identity, bias=nt1[:, t:t + 1],
                                         scale=rstd[:, t:t + 1]).then_inc(s_ctd, 1)

            def copy_expert_rows(f):
                for c in range(NC):
                    act.wait_ge(s_fp, f * N_FP + c + 1)
                    copy(xn_t[:, c, :], fb[c][:, :]).then_inc(s_fc, 1)

            def batch(i, f):
                copy_rows(i, 0)
                split_high(i, 0)
                attention(i, f, 0)
                copy_rows(i, 1)
                centre(i)
                copy_rows(i, 2)
                act.wait_ge(s_c, i + 1)
                copy(c_t[:, :], st[0][:, :]).then_inc(s_cc, 1)
                split_high(i, 1)
                attention(i, f, 1)
                copy_rows(i, 3)

            for r in range(8):
                act.wait_ge(s_wt, r + 1)
                dst = win_t[:, :, r * P:(r + 1) * P] if r < 6 else wout_t[:, :, (r - 6) * P:(r - 5) * P]
                copy(dst, tri[r % 3][:, 0:NC * P].rearrange("p (c q) -> p c q", c=NC)).then_inc(s_wc, 1)
            act.wait_ge(s_fill, 2)
            batch(0, None)
            with act.Fori(1, B) as i:
                batch(i, i - 1)
            copy_expert_rows(B - 1)
            for n in range(2 * NH):
                tanh(B - 1, n)
                for k in range(2 if n == 0 else 0):
                    gate_exp(B - 1, k)
                if n > NH:
                    hidden_high(B - 1, n - 1)
            hidden_high(B - 1, 2 * NH - 1)

        @block.tensor
        def _(pe):
            mm = nc.tensor.matmul

            def transpose_rows(src, banks, signal):
                for c in range(NC):
                    for t in range(NT):
                        last = nc.tensor.transpose(banks[c][:, t * P:(t + 1) * P], src[:, t, c * P:(c + 1) * P], ident[:, :])
                    last.then_inc(signal, 1)

            def project_rows(dst, w, src_t, t):
                for c in range(NC):
                    last = mm(dst, src_t[:, c, t * P:(t + 1) * P], w[:, c, :], start=(c == 0), stop=(c == NC - 1))
                return last

            def stacks(i, a, t):
                pe.wait_ge(s_lo, i * N_LO + a * NT + t + 1)
                for k in range(4):
                    before = 4 * t + k - 3
                    if before >= 0:
                        read = a * 8 + before // 2 + 1
                        if before % 2 == 0:
                            pe.wait_ge(s_sa, i * N_SA + read)
                        else:
                            pe.wait_ge(s_sd, i * N_SD + read)
                    for b in range(4):
                        pr = 2 * (4 * k + b)
                        last = nc.tensor.transpose(
                            stack_bank(a, t, k)[:, b * P:(b + 1) * P],
                            stack[:, t % 2, pr:pr + 2, :].bitcast(F32).rearrange("p h s -> p (h s)"), ident[:, :])
                    last.then_inc(s_sp, 1)

            def max_unit(i, a, g, n):
                t, h = n // GH, g * GH + n % GH
                u = (a * NGR + g) * UNITS + n
                r, b = SK * (h % 2), h // 2
                lo, hi = kcols(t, a)
                w = g * UNITS + n
                if w >= 2 and w - LEAD_WIDE.start not in (2, 3):
                    back = 4 if w - 4 in LEAD_WIDE and w in LEAD_WIDE else 2
                    pe.wait_ge(s_mx, i * N_MX + u - back + 1)
                last = mm(max_bank(w)[:, 0:hi - lo], q_t[r:r + MROW, b, t * P:(t + 1) * P], k_t[r:r + MROW, b, lo:hi],
                          start=True, stop=(a == 1))
                if a == 0:
                    last = mm(max_bank(w)[:, 0:hi - lo], identb[:, :], mask_qk[:, BACK * P - (hi - lo):BACK * P],
                              start=False, stop=True)
                last.then_inc(s_sm, 1)

            def max_rows(i, a, g):
                pe.wait_ge(s_ms, i * N_MS + a * NGR + g + 1)
                if g >= 2:
                    pe.wait_ge(s_on, i * N_ON + a * NGR + g - 1)
                for t in range(NT):
                    last = nc.tensor.transpose(
                        dn[0:8, t * P:(t + 1) * P],
                        m_split[:, g % 2, t].bitcast(F32).rearrange("p h j b -> p (h j b)"), ident[:, :])
                last.then_inc(s_mp, 1)

            def score_unit(i, a, g, n):
                j, h = n // GH, g * GH + n % GH
                u = (a * NGR + g) * UNITS + n
                r, b = SK * (h % 2), h // 2
                lo, hi = qcols(j, a)
                if n == 0:
                    pe.wait_ge(s_mr[g % 2], i * N_MR + 64 * (a * NGR // 2 + g // 2 + 1))
                w = g * UNITS + n
                if w >= 2 and w - TAIL_WIDE not in (2, 3):
                    back = 4 if w - 4 >= TAIL_WIDE else 2
                    pe.wait_ge(s_ex, i * N_EX + u - back + 1)
                last = mm(score_bank(w)[:, 0:hi - lo], k_t[r:r + SK, b, j * P:(j + 1) * P], q_t[r:r + SK, b, lo:hi],
                          start=True, stop=(a == 1))
                if a == 0:
                    last = mm(score_bank(w)[:, 0:hi - lo], identb[:, :], mask_kq[:, 0:hi - lo], start=False, stop=True)
                last.then_inc(s_st, 1)

            def weigh(i, a, g, j):
                lo, hi = qcols(j, a)
                if j == 0 and g >= 1:
                    pe.wait_ge(s_oc, i * N_OC + a * NGR + g)
                for c in range(GH):
                    n = j * GH + c
                    pe.wait_ge(s_ex, i * N_EX + (a * NGR + g) * UNITS + n + 1)
                    last = mm(ot[VW * c:VW * (c + 1), lo:hi], v_s[:, j, g * GH + c, :], probs[:, n % PSLOTS, 0:hi - lo],
                              start=(j == 0), stop=(j == NT - 1), skip_group_check=True)
                last.then_inc(s_pv, 1)

            def outputs(i, a, g):
                pe.wait_ge(s_oc, i * N_OC + a * NGR + g + 1)
                last_rows = min(g + 1, NGR - 1)
                pe.wait_ge(s_mc, i * N_MC + a * NGR + last_rows + 1)
                if g == NGR - 1:
                    pe.wait_ge(s_on, i * N_ON + a * NGR + g)
                for t in range(NT):
                    last = nc.tensor.transpose(dn[:, t * P:(t + 1) * P], o_t[:, t * P:(t + 1) * P], ident[:, :])
                last.then_inc(s_op, 1)

            def hidden(f, s):
                n, half, c = s // 4, s // 2 % 2, s % 2
                u, m = n // NH, n % NH
                if s == 0:
                    pe.wait_ge(s_gr, f + 1)
                elif n >= 1 and c == 0 and half == 0:
                    pe.wait_ge(s_sg, f * N_SG + n)
                elif n >= 1 and c == 0 and half == 1:
                    pe.wait_ge(s_ht, f * N_HT + n)
                col = half * HID + m * P
                product = mm(fb[half][:, :], wup_s[:, u, c, col:col + P], xn_t[:, c, :], start=(c == 0), stop=(c == NC - 1))
                if c == NC - 1:
                    product.then_inc((s_up, s_ub)[half], 1)

            def expert_out(f, q, m):
                k, t = divmod(q - NT, NT)
                rows = slice(t * P, (t + 1) * P)
                if m == 0:
                    if q == 0:
                        pe.wait_ge(s_ht, f * N_HT + 2 * NH)
                    if q == NT:
                        pe.wait_ge(s_hl, f * N_HL + NH)
                    if q >= 2:
                        pe.wait_ge(s_er, f * N_ER + q - 1)
                    if q >= NT and t == 0:
                        pe.wait_ge(s_w2[k % 2], f * N_W2 + 16 * (k // 2 + 1))
                if q < NT:
                    last = mm(fb[q % 2][:, 0:E], h_s[:, m, rows], wso_s[:, m, :], start=(m == 0), stop=(m == NH - 1))
                else:
                    for n, (h, w) in enumerate(((0, 0), (0, 1), (1, 0))):
                        last = mm(fb[q % 2][:, :], h_r[:, h, m, rows], w2_r[:, k % 2, w, m, :],
                                  start=(m == 0 and n == 0), stop=(m == NH - 1 and n == 2))
                if m == NH - 1:
                    last.then_inc(s_eo, 1)

            def out_rows(f, q):
                for m in range(NH):
                    expert_out(f, q, m)

            def experts_rows(f, e):
                pe.wait_ge(s_x2, f + 1)
                if e is not None:
                    pe.wait_ge(s_er, (e + 1) * N_ER)
                transpose_rows(x2, fb, s_fp)

            def gate_logits(f):
                pe.wait_ge(s_fc, (f + 1) * N_FC)
                for t in range(NT):
                    last = project_rows(fb[0][:, t * 16:t * 16 + NG + NE], wgate_s, xn_t, t)
                last.then_inc(s_gl, 1)

            def attention(i, f, e, a):
                for m in range(-LEAD, ALL):
                    if a == 0 and m == LAST_STACKS_AT:
                        stacks(i, a, NT - 1)
                    if m + LEAD < UNITS and (m + LEAD) % GH == 0:
                        tiles = max(NT - 1, (m + LEAD) // GH + 1) if a == 0 else NT
                        pe.wait_ge(s_sa, i * N_SA + a * 8 + 2 * tiles)
                        pe.wait_ge(s_sd, i * N_SD + a * 8 + 2 * tiles)
                    if m + LEAD < ALL:
                        max_unit(i, a, *divmod(m + LEAD, UNITS))
                    if m >= 0:
                        g, n = divmod(m, UNITS)
                        if n == 0 and g >= 1:
                            weigh(i, a, g - 1, NT - 1)
                        score_unit(i, a, g, n)
                        if n % GH == 2 and n > GH:
                            weigh(i, a, g, n // GH - 1)
                        if n == 3 and g >= 1:
                            outputs(i, a, g - 1)
                    if (m + LEAD) % UNITS == ROWS_AT and UNITS < m + LEAD < ALL + UNITS:
                        max_rows(i, a, (m + LEAD) // UNITS - 1)
                    if f is not None and a == 0:
                        if m == ROWS_FROM:
                            experts_rows(f, e)
                        if m == LOGITS_AT:
                            gate_logits(f)
                        for s in range(8 * NH):
                            if HIDDEN_AT[s] == m:
                                hidden(f, s)
                    if f is not None and a == 1:
                        for s in range(len(OUT_AT)):
                            if OUT_AT[s] == m:
                                expert_out(f, OUT_BESIDE[s // NH], s % NH)
                weigh(i, a, NGR - 1, NT - 1)
                beside_end(f, a, 0)
                outputs(i, a, NGR - 1)
                beside_end(f, a, 1)

            def beside_end(f, a, part):
                if f is not None:
                    for q, m in OUT_END[a][part]:
                        expert_out(f, q, m)

            def project_attention(i, f, a, w):
                pe.wait_ge(s_on, i * N_ON + (a + 1) * NGR)
                transpose_rows(o_s, pair, s_tp)
                beside_end(f, a, 2)
                pe.wait_ge(s_tc, i * N_TC + (2 + 2 * a) * NC)
                for m in range(2):
                    for t in (2 * m, 2 * m + 1):
                        last = project_rows(st[m][:, (t % 2) * E:(t % 2 + 1) * E], w, xn_t, t)
                    last.then_inc(s_pj, 1)

            def heads(i, a, f):
                def beside(t):
                    if f is not None:
                        for q in OUT_HEADS[a][t]:
                            out_rows(f, q)

                for t in range(NT):
                    if t >= 2:
                        pe.wait_ge(s_rp, i * N_RP + a * NT + t - 1)
                    if a == 0:
                        project_rows(pair[t % 2][:, :], win_t[:, :, 0:2 * E], xn_t, t).then_inc(s_qk, 1)
                    else:
                        project_rows(pair[t % 2][:, 0:E], wq_s, xn_t, t)
                        if t == 0:
                            pe.wait_ge(s_cc, i + 1)
                        mm(pair[t % 2][:, E:2 * E], c_t[0:DC, t * P:(t + 1) * P], wkv_s[0:DC, :],
                           start=True, stop=True).then_inc(s_qk, 1)
                    if t >= 1:
                        pe.wait_ge(s_vc, i * N_VC + a * NT + t)
                    if a == 0:
                        project_rows(vb[:, 0:E], win_t[:, :, 2 * E:3 * E], xn_t, t).then_inc(s_v, 1)
                    else:
                        mm(vb[:, 0:E], c_t[DC:2 * DC, t * P:(t + 1) * P], wkv_s[DC:2 * DC, :],
                           start=True, stop=True).then_inc(s_v, 1)
                    if t >= 2:
                        stacks(i, a, t - 2)
                    beside(t)
                stacks(i, a, NT - 2)
                beside(NT)
                if a == 1:
                    stacks(i, a, NT - 1)

            def batch(i, f, e):
                pe.wait_ge(s_xa, i + 1)
                transpose_rows(xa, pair, s_tp)
                pe.wait_ge(s_tc, i * N_TC + NC)
                if f is not None:
                    pe.wait_ge(s_pr, i * N_PR)
                heads(i, 0, e)
                if f is None:
                    pe.wait_ge(s_w, 16 * N_LOADS)
                attention(i, f, e, 0)
                project_attention(i, f, 0, wout_t)
                if f is not None:
                    for q in OUT_FIRST:
                        out_rows(f, q)
                pe.wait_ge(s_xn, i + 1)
                transpose_rows(xn, pair, s_tp)
                pe.wait_ge(s_tc, i * N_TC + 3 * NC)
                for c in range(NC):
                    last = mm(st[0][:, :], wc_s[:, c, :], xn_t[:, c, :], start=(c == 0), stop=(c == NC - 1))
                last.then_inc(s_c, 1)
                heads(i, 1, f)
                attention(i, f, e, 1)
                project_attention(i, f, 1, wo_s)

            pe.wait_ge(s_const, 5)
            pe.wait_ge(s_w1, 16 * N_FIRST_LOADS)
            for r in range(8):
                if r >= 3:
                    pe.wait_ge(s_wc, r - 2)
                for c in range(NC):
                    last = nc.tensor.transpose(tri[r % 3][:, c * P:(c + 1) * P], w_raw[:, r, c * P:(c + 1) * P], ident[:, :])
                last.then_inc(s_wt, 1)
            pe.wait_ge(s_wc, 8)
            batch(0, None, None)
            batch(1, 0, None)
            with pe.Fori(2, B) as i:
                batch(i, i - 1, i - 2)
            for q in sum(OUT_HEADS[0], ()):
                out_rows(B - 2, q)
            experts_rows(B - 1, B - 2)
            gate_logits(B - 1)
            for s in range(8 * NH):
                hidden(B - 1, s)
            for q in range(OUTS):
                out_rows(B - 1, q)

        @block.vector
        def _(dve):
            v = nc.vector
            steps = [0]

            def done(ins):
                ins.then_inc(s_dve, 1)
                steps[0] += 1
                dve.wait_ge(s_dve, steps[0])

            def count_anew():
                dve.sem_clear(s_dve)
                steps[0] = 0

            def signal(ins):
                ins.then_inc(s_dve, 1)
                steps[0] += 1

            def settle():
                dve.wait_ge(s_dve, steps[0])

            def run(steps_of):
                for _ in steps_of:
                    pass

            def moments(rows):
                for t in range(NT):
                    signal(v.bn_stats(stats[:, t, :], rows(t)))
                    yield
                settle()
                for t in range(NT):
                    last = v.bn_aggr(mv[:, t, :], stats[:, t, :])
                signal(last)
                yield

            def inverse_root():
                settle()
                signal(v.tensor_scalar(bits[:, :], var[:, :].bitcast(I32), 1, None, ALU.logical_shift_right))
                yield
                settle()
                signal(v.tensor_scalar(rstd[:, :].bitcast(I32), bits[:, :], -1.0, RSQRT_MAGIC, ALU.mult, ALU.add))
                yield
                for _ in range(3):
                    settle()
                    signal(v.tensor_tensor(nt1[:, :], rstd[:, :], rstd[:, :], ALU.mult))
                    yield
                    settle()
                    signal(v.scalar_tensor_tensor(nt2[:, :], nt1[:, :], -0.5, var[:, :], ALU.mult, ALU.mult))
                    yield
                    settle()
                    signal(v.scalar_tensor_tensor(rstd[:, :], nt2[:, :], 1.5, rstd[:, :], ALU.add, ALU.mult))
                    yield

            def layer_scale():
                settle()
                signal(v.tensor_scalar(var[:, :], mv[:, :, 1], LN_EPS, None, ALU.add))
                yield
                yield from inverse_root()

            def rms_scale():
                settle()
                signal(v.tensor_tensor(nt1[:, :], mv[:, :, 0], mv[:, :, 0], ALU.mult))
                yield
                settle()
                signal(v.scalar_tensor_tensor(var[:, :], nt1[:, :], RMS_EPS, mv[:, :, 1], ALU.add, ALU.add))
                yield
                yield from inverse_root()

            def centre(dst, rows, t):
                settle()
                return v.tensor_scalar(dst, rows, mv[:, t, 0:1], rstd[:, t:t + 1], ALU.subtract, ALU.mult)

            def weight(rows, t, norm):
                settle()
                return v.scalar_tensor_tensor(rows, rows, rstd[:, t:t + 1], norm_w[:, norm, :], ALU.mult, ALU.mult)

            def rotate(i, a, t):
                bf, n = t % 2, a * NT + t
                dve.wait_ge(s_qk, i * N_QK + n + 1)
                if t >= 2:
                    dve.wait_ge(s_lo, i * N_LO + n - 1)
                if t >= 1:
                    dve.wait_ge(s_rot, i * N_ROT + n)
                src = pair[t % 2][:, :].rearrange("p (h d) -> p h d", d=D)
                pairs = pair[t % 2][:, :].rearrange("p (h f o) -> p h f o", f=D // 2, o=2)
                cross = rot_b[:, :, :].rearrange("p h (f o) -> p h f o", o=2)
                sin = rope_sin[:, a, t].rearrange("p (o f) -> p o f", o=2)
                v.tensor_tensor(rot[:, bf], src, rope_cos[:, a, t:t + 1, :].to_broadcast([P, 2 * H, D]), ALU.mult)
                for o in range(2):
                    last = v.tensor_tensor(cross[:, :, :, o], pairs[:, :, :, 1 - o],
                                           sin[:, o:o + 1, :].to_broadcast([P, 2 * H, D // 2]), ALU.mult)
                last.then_inc(s_rp, 1)
                dve.wait_ge(s_rp, i * N_RP + n + 1)
                v.tensor_tensor(rot[:, bf], rot[:, bf], rot_b[:, :, :], ALU.add).then_inc(s_rot, 1)

            def copy_stacks(i, a, t):
                for k, dst in ((1, q_t), (3, k_t)):
                    dve.wait_ge(s_sp, i * N_SP + a * 16 + 4 * t + k + 1)
                    v.tensor_copy(dst[:, 4:8, t * P:(t + 1) * P],
                                  stack_bank(a, t, k)[:, :].rearrange("p (b q) -> p b q", b=4)).then_inc(s_sd, 1)

            def take_max(i, a, g, n):
                u = (a * NGR + g) * UNITS + n
                lo, hi = kcols(n // GH, a)
                dve.wait_ge(s_sm, i * N_SM + u + 1)
                return v.tensor_reduce(negmax[:, g % 2, n // GH, n % GH:n % GH + 1],
                                       max_bank(g * UNITS + n)[:, 0:hi - lo], AX.X,
                                       ALU.max, negate=True).then_inc(s_mx, 1)

            def split_max(i, a, g):
                dve.wait_ge(s_mx, i * N_MX + (a * NGR + g + 1) * UNITS)
                if g >= 2:
                    dve.wait_ge(s_mp, i * N_MP + a * NGR + g - 1)
                m = negmax[:, g % 2].rearrange("p t (b h) -> p t h b", b=2)
                hi = m_split[:, g % 2, :, :, 0, :]
                lo = m_split[:, g % 2, :, :, 1, :]
                done(v.tensor_copy(hi, m))
                v.tensor_tensor(lo, m, hi.bitcast(F32), ALU.subtract).then_inc(s_ms, 1)

            def normalise(i, a, g):
                dve.wait_ge(s_op, i * N_OP + a * NGR + g + 1)
                o = dn[:, :].rearrange("p (t h w) -> p t h w", t=NT, h=GH)
                done(v.reciprocal(den[:, :, :], o[:, :, :, D]))
                if a == 1 and g == 0:
                    dve.wait_ge(s_xk, 16 * (i + 1))
                for t in range(NT):
                    last = v.tensor_tensor(
                        o_s[:, t, g * GH * D:(g + 1) * GH * D].rearrange("p (h d) -> p h d", h=GH), o[:, t, :, 0:D],
                        den[:, t].rearrange("p (h o) -> p h o", o=1).to_broadcast([P, GH, D]), ALU.mult)
                last.then_inc(s_on, 1)


            def heads(i, a, beside):
                rotate(i, a, 0)
                for t in range(NT):
                    if t + 1 < NT:
                        rotate(i, a, t + 1)
                    beside(t)
                    if t >= 1:
                        copy_stacks(i, a, t - 1)
                beside(NT)
                if a == 1:
                    copy_stacks(i, a, NT - 1)

            def attention(i, f, e, a, more):
                def beside():
                    if f is not None and a == 0:
                        yield from gates(f)
                    if e is not None and a == 0:
                        yield from finish(e)
                    if a == 1 and more:
                        yield from first_source(i + 1)

                others, begin = beside(), (GATES_FROM, SOURCE_FROM)[a]
                for m in range(-LEAD, ALL):
                    if a == 0 and m == LAST_STACKS_AT:
                        copy_stacks(i, a, NT - 1)
                    if m + LEAD < ALL:
                        take_max(i, a, *divmod(m + LEAD, UNITS))
                    if (m + LEAD) % UNITS == UNITS - 1 and m + LEAD < ALL:
                        split_max(i, a, (m + LEAD) // UNITS)
                    if m >= UNITS and m % UNITS == 4:
                        normalise(i, a, m // UNITS - 1)
                    if f is not None and a == 0:
                        for n in range(2 * NH):
                            if HIDDEN_AT[4 * n + 1] + DVE_LAG == m:
                                gated_half(f, n)
                            if HIDDEN_AT[4 * n + 3] + DVE_LAG == m:
                                hidden(f, n)
                    if f is not None and a == 1:
                        for k, q in enumerate(OUT_BESIDE):
                            if OUT_AT[NH * k + NH - 1] + DVE_LAG == m:
                                expert_out(f, q)
                    if m >= begin:
                        next(others, None)
                run(others)
                normalise(i, a, NGR - 1)
                out_now(f, sorted({q for part in OUT_END[a] for q, m in part}))

            def first_source(i):
                dve.wait_ge(s_x, i * 16 + 16)
                yield from moments(lambda t: x_s[:, t, :])
                yield from layer_scale()
                for t in range(NT):
                    last = centre(xa[:, t, :], x_s[:, t, :], t)
                    if t + 1 < NT:
                        yield
                last.then_inc(s_xa, 1)

            def gates(i):
                dve.wait_ge(s_gl, i + 1)
                lg = fb[0][:, 0:NT * 16].rearrange("p (t n) -> p t n", t=NT)[:, :, 0:NG + NE]
                v.tensor_tensor(logit[:, :, :], lg,
                                bias_s[:, :].rearrange("p (o n) -> p o n", o=1).to_broadcast([P, NT, NG + NE]),
                                ALU.add).then_inc(s_gr, 1)
                yield
                dve.wait_ge(s_gr, i + 1)
                signal(v.tensor_tensor(gd[:, :], logit[:, :, 1], logit[:, :, 0], ALU.subtract))
                signal(v.tensor_copy(esel[:, :, :], logit[:, :, NG:NG + EPG]))
                yield
                settle()
                signal(v.tensor_scalar(gsel[:, :], gd[:, :], 0.0, None, ALU.is_gt))
                signal(v.tensor_scalar(nt1[:, :], gd[:, :], -1.0, None, ALU.mult))
                yield
                settle()
                sel = gsel[:, :].rearrange("p (t o) -> p t o", o=1).to_broadcast([P, NT, EPG])
                signal(v.tensor_copy(ediff[:, :, :], sel))
                v.tensor_tensor(gabs[:, :], gd[:, :], nt1[:, :], ALU.min).then_inc(s_ge, 1)
                yield
                settle()
                signal(v.copy_predicated(esel[:, :, :], ediff[:, :, :].bitcast(I32), logit[:, :, NG + EPG:NG + NE]))
                yield
                settle()
                signal(v.tensor_reduce(emax[:, :], esel[:, :, :], AX.X, ALU.max))
                yield
                settle()
                v.tensor_tensor(esub[:, :, :], esel[:, :, :],
                                emax[:, :].rearrange("p (t o) -> p t o", o=1).to_broadcast([P, NT, EPG]),
                                ALU.subtract).then_inc(s_ge, 1)
                for t in range(NT):
                    one = esel[:, t].rearrange("p (e o) -> p e o", o=1).to_broadcast([P, EPG, EPG])
                    other = esel[:, t:t + 1, :].to_broadcast([P, EPG, EPG])
                    v.tensor_tensor(egt[:, t], other, one, ALU.is_gt)
                    signal(v.tensor_tensor(eeq[:, t], other, one, ALU.is_equal))
                    yield
                settle()
                for t in range(NT):
                    signal(v.tensor_tensor(eeq[:, t], eeq[:, t], lower[:, :, :], ALU.mult))
                    if t % 2 == 1:
                        yield
                settle()
                signal(v.tensor_tensor(egt[:, :, :, :], egt[:, :, :, :], eeq[:, :, :, :], ALU.add))
                yield
                settle()
                signal(v.tensor_reduce(rank[:, :, :], egt[:, :, :, :], AX.X, ALU.add))
                yield
                dve.wait_ge(s_gx, i * N_GX + 2)
                signal(v.tensor_scalar(gprob[:, :], gexp[:, :], 1.0, None, ALU.add))
                signal(v.tensor_reduce(esum[:, :], eexp[:, :, :], AX.X, ALU.add))
                yield
                settle()
                signal(v.tensor_tensor(gprob[:, :], gprob[:, :], esum[:, :], ALU.mult))
                yield
                settle()
                signal(v.reciprocal(gprob[:, :], gprob[:, :]))
                signal(v.scalar_tensor_tensor(ew[:, :, :], rank[:, :, :], 2.0, eexp[:, :, :], ALU.is_lt, ALU.mult))
                yield
                settle()
                signal(v.tensor_tensor(ew[:, :, :], ew[:, :, :],
                                       gprob[:, :].rearrange("p (t o) -> p t o", o=1).to_broadcast([P, NT, EPG]),
                                       ALU.mult))
                yield
                settle()
                signal(v.tensor_tensor(gate[:, :, EPG:NE], ew[:, :, :], sel, ALU.mult))
                yield
                settle()
                signal(v.tensor_tensor(gate[:, :, 0:EPG], ew[:, :, :], gate[:, :, EPG:NE], ALU.subtract))
                yield

            def gated_half(f, n):
                dve.wait_ge(s_th, f * N_TH + n + 1)
                if NH + 2 <= n:
                    dve.wait_ge(s_hl, f * N_HL + n - 2 - NH + 1)
                elif n >= 2:
                    dve.wait_ge(s_ht, f * N_HT + n - 1)
                v.scalar_tensor_tensor(sg[:, n % 2, :], th[:, :], 1.0, fb[0][:, :], ALU.add,
                                       ALU.mult).then_inc(s_sg, 1)

            def hidden(f, n):
                dve.wait_ge(s_sg, f * N_SG + n + 1)
                dve.wait_ge(s_ub, f * N_UB + n + 1)
                block = h_s[:, n, :] if n < NH else sg[:, n % 2, :]
                v.scalar_tensor_tensor(block, sg[:, n % 2, :], 0.5, fb[1][:, :], ALU.mult, ALU.mult).then_inc(s_ht, 1)

            def expert_out(f, q):
                dve.wait_ge(s_eo, f * N_EO + q + 1)
                if q < NT:
                    if q == 0:
                        dve.wait_ge(s_yfree, 16 * (f + 1))
                    v.tensor_tensor(acc[:, q, :], fb[q % 2][:, 0:E], x2[:, q, :], ALU.add).then_inc(s_er, 1)
                    return
                if q == NT:
                    settle()
                k, t = divmod(q - NT, NT)
                dve.wait_ge(s_er, f * N_ER + q)
                for e in (2 * k, 2 * k + 1):
                    add = v.scalar_tensor_tensor(acc[:, t, :], fb[q % 2][:, (e % 2) * E:(e % 2 + 1) * E],
                                                 gate[:, t, e:e + 1], acc[:, t, :], ALU.mult, ALU.add)
                    if e % 2 == 0:
                        done(add)
                add.then_inc(s_er, 1)

            def finish(f):
                dve.wait_ge(s_er, (f + 1) * N_ER)
                yield from moments(lambda t: acc[:, t, :])
                yield from rms_scale()
                for t in range(NT):
                    signal(weight(acc[:, t, :], t, 1))
                    yield
                settle()
                yield from moments(lambda t: acc[:, t, :])
                yield from layer_scale()
                for t in range(NT):
                    signal(centre(acc[:, t, :], acc[:, t, :], t))
                    yield
                settle()
                dve.wait_ge(s_xb, 16 * (f + 1))
                for t in range(NT):
                    last = v.tensor_tensor(acc[:, t, :], acc[:, t, :], x1_back[:, t, :], ALU.add)
                    if t + 1 < NT:
                        yield
                last.then_inc(s_y, 1)
                yield

            def expert_source(f):
                yield from moments(lambda t: x2[:, t, :])
                yield from rms_scale()
                for t in range(NT):
                    last = weight(x2[:, t, :], t, 0)
                    if t + 1 < NT:
                        yield
                last.then_inc(s_x2, 1)

            def out_now(f, outs):
                if f is not None:
                    for q in outs:
                        expert_out(f, q)

            def weave(steps_of, f, outs):
                for k, _ in enumerate(steps_of):
                    if k % 4 == 3:
                        out_now(f, outs[k // 4:k // 4 + 1])

            def batch(i, f, e, more):
                source = expert_source(f) if f is not None else iter(())

                def beside_first(t):
                    out_now(e, OUT_HEADS[0][t])
                    for _ in range(SOURCE_STEPS):
                        next(source, None)

                def beside_second(t):
                    out_now(f, OUT_HEADS[1][t])

                heads(i, 0, beside_first)
                run(source)
                attention(i, f, e, 0, more)
                dve.wait_ge(s_pj, i * N_PJ + 2)
                run(moments(projected))
                weave(layer_scale(), f, OUT_FIRST[0:1])
                settle()
                v.scalar_tensor_tensor(nt1[:, :], mv[:, :, 0], -1.0, rstd[:, :], ALU.mult, ALU.mult).then_inc(s_ctr, 1)
                out_now(f, OUT_FIRST[1:2])
                for t in range(NT):
                    dve.wait_ge(s_ctd, i * NT + t + 1)
                    last = v.tensor_tensor(x1[:, t, :], x_s[:, t, :], x1[:, t, :], ALU.add)
                    if t < NT - 1:
                        signal(last)
                last.then_inc(s_res, 1)
                settle()
                dve.wait_ge(s_res, i + 1)
                v.memset(spare[:, :], 0.0).then_inc(s_pr, 1)
                run(moments(lambda t: x1[:, t, :]))
                weave(layer_scale(), f, OUT_FIRST[2:4])
                for t in range(NT):
                    last = centre(xn[:, t, :], x1[:, t, :], t)
                last.then_inc(s_xn, 1)
                out_now(f, OUT_FIRST[4:])
                heads(i, 1, beside_second)
                attention(i, f, e, 1, more)
                dve.wait_ge(s_pj, i * N_PJ + 4)
                for t in range(NT):
                    last = v.tensor_tensor(x2[:, t, :], projected(t), xn[:, t, :], ALU.add)
                last.then_inc(s_pr, 1)
                dve.wait_ge(s_pr, (i + 1) * N_PR)

            v.memset(v_s[:, :, :, :], 0.0)
            done(v.memset(stack[:, :, :, :].bitcast(F32), 0.0))
            v.memset(v_s[:, :, :, D:D + 1], 1.0).then_inc(s_fill, 1)
            v.memset(stack[:, :, H:2 * H, MROW:MROW + 2].bitcast(F32), 1.0).then_inc(s_fill, 1)
            v.memset(spare[:, :], 0.0).then_inc(s_yfree, 16)
            dve.wait_ge(s_yfree, 16)
            dve.wait_ge(s_w1, 16 * N_FIRST_LOADS)
            dve.wait_ge(s_const, 5)
            run(first_source(0))
            batch(0, None, None, True)
            dve.wait_ge(s_w, 16 * N_LOADS)
            dve.wait_ge(s_w2l, NE)
            batch(1, 0, None, True)
            with dve.Fori(2, B - 1) as i:
                count_anew()
                batch(i, i - 1, i - 2, True)
            count_anew()
            batch(B - 1, B - 2, B - 3, False)
            source = expert_source(B - 1)
            for q in sum(OUT_HEADS[0], ()):
                out_now(B - 2, (q,))
                for _ in range(SOURCE_STEPS):
                    next(source, None)
            run(source)

            def beside_last():
                yield from gates(B - 1)
                yield from finish(B - 2)

            others = beside_last()
            next(others)
            for n in range(2 * NH):
                gated_half(B - 1, n)
                hidden(B - 1, n)
                for _ in range(STEPS_AT_LAST):
                    next(others, None)
            run(others)
            out_now(B - 1, range(OUTS))
            run(finish(B - 1))


def rope_tables():
    ts = np.arange(T, dtype=np.float32)[:, None]
    ds = np.arange(D // 2, dtype=np.float32)
    out = np.zeros((2, 2, T, D), np.float32)
    for a, freqs in enumerate((np.exp(ds * np.float32(-np.log(10000.0) * 2.0 / D)),
                               np.float32(1.0) / np.float32(10000.0) ** (np.arange(0, D, 2, dtype=np.float32) / D))):
        angle = ts * freqs.astype(np.float32)[None, :]
        out[a, 0] = np.repeat(np.cos(angle), 2, axis=1)
        out[a, 1] = np.concatenate([-np.sin(angle), np.sin(angle)], axis=1)
    return np.ascontiguousarray(out.reshape(2, 2, NT, P, D).transpose(1, 3, 0, 2, 4))


_INS = ["L0_attn_query", "L0_attn_in_proj_w", "L0_attn_out_proj_w", "L0_ffn_Wq", "L0_ffn_Wk_c", "L0_ffn_Wv_c",
        "L0_ffn_Wk", "L0_ffn_Wv", "L0_ffn_Wo", "L0_ffn_W_shared_in", "L0_ffn_W_shared_out", "L0_ffn_W1_shared",
        "L0_ffn_W2_experts", "L0_ffn_Wg_gate", "L0_ffn_We_gate", "L0_ffn_group_bias", "L0_ffn_expert_bias",
        "L0_ffn_norm1_w", "L0_ffn_norm2_w"]


def kernel(**inputs):
    import concourse.bacc as bacc
    from concourse.bass_utils import run_bass_kernel_spmd

    nc = bacc.Bacc("TRN2", target_bir_lowering=False, num_devices=1)
    arrays = {f"in_{n}": np.ascontiguousarray(inputs[n]) for n in _INS}
    arrays["in_rope"] = rope_tables()
    args = [nc.dram_tensor(n, a.shape, mybir.dt.from_np(a.dtype), kind="ExternalInput").ap() for n, a in arrays.items()]
    out = nc.dram_tensor("out_0", (B, T, E), F32, kind="ExternalOutput").ap()
    build(nc, *args, out)
    r = run_bass_kernel_spmd(nc, [arrays], core_ids=[0])
    return r.results[0]["out_0"]
```
